# Optimizing a Trainium2 kernel written in Bass

```python
import numpy as np
import jax
import jax.numpy as jnp

def _softmax(x, axis=-1):
    return jax.nn.softmax(x, axis=axis)

def _gelu(x):
    return jax.nn.gelu(x, approximate=True)

def _silu(x):
    return jax.nn.silu(x)

def _sigmoid(x):
    return jax.nn.sigmoid(x)

def _layernorm(x, axis=-1, eps=1e-05):
    m = jnp.mean(x, axis=axis, keepdims=True)
    v = jnp.var(x, axis=axis, keepdims=True)
    return (x - m) / jnp.sqrt(v + eps)

def _scatter_add(tgt, idx, src, axis=0):
    return tgt.at[idx].add(src)

def _segment_sum(src, seg, n):
    return jax.ops.segment_sum(src, seg, n)
kernel_name = 'mk_early_fusion_d1_tok_img768_r4_dcd766'

def setup_inputs(seed: int=0):
    np.random.seed(seed)
    _w = jnp.asarray

    def _rec_inputs():
        import jax
        import jax.numpy as jnp
        _rk = jax.random.key(seed)
        x = -0.00016672 + 0.999947 * jax.random.normal(jax.random.fold_in(_rk, 1), (16, 3, 128, 128), jnp.float32)
        txt = -1.41974e-10 + 0.999985 * jax.random.normal(jax.random.fold_in(_rk, 2), (16, 77, 192), jnp.float32)
        return (x, txt)
    x, txt = _rec_inputs()

    def _L0_tok_setup():
        import jax, jax.numpy as jnp
        import numpy as np
        P = 16
        EPS = 1e-05
        key = jax.random.key(seed)
        k1, k2, k3, k4, k5 = jax.random.split(key, 5)
        B, C, H, W = (64, 3, 96, 96)
        d_in = C * P * P
        h_dim = 192
        x = jax.random.normal(k1, (B, C, H, W), dtype=jnp.float32)
        bound = 1.0 / np.sqrt(d_in)
        W_proj = jax.random.uniform(k2, (h_dim, d_in), jnp.float32, -bound, bound)
        b_proj = jax.random.uniform(k3, (h_dim,), jnp.float32, -bound, bound)
        gamma = jnp.ones((h_dim,), jnp.float32)
        beta = jnp.zeros((h_dim,), jnp.float32)
        return {'x': x, 'W_proj': W_proj, 'b_proj': b_proj, 'gamma': gamma, 'beta': beta}
    _L0_tok_all = _L0_tok_setup()
    _L0_tok_in = {k: v for k, v in _L0_tok_all.items() if k in ('W_proj', 'b_proj', 'gamma', 'beta')}
    del _L0_tok_all

    def _L0_attn_setup():
        import jax, jax.numpy as jnp
        import numpy as np
        D_MODEL = 192
        D_STATE = 16
        EXPAND = 2
        D_INNER = EXPAND * D_MODEL
        DT_RANK = D_MODEL // 16
        D_CONV = 4
        BATCH = 2
        SEQ = 256

        def _init_params(key, prefix):
            ks = jax.random.split(key, 6)
            s = 0.02
            p = {}
            p[prefix + '_in_w'] = jax.random.normal(ks[0], (2 * D_INNER, D_MODEL), dtype=jnp.float32) * s
            p[prefix + '_conv_w'] = jax.random.normal(ks[1], (D_INNER, D_CONV), dtype=jnp.float32) * s
            p[prefix + '_conv_b'] = jnp.zeros((D_INNER,), dtype=jnp.float32)
            p[prefix + '_xproj_w'] = jax.random.normal(ks[2], (DT_RANK + 2 * D_STATE, D_INNER), dtype=jnp.float32) * s
            p[prefix + '_dt_w'] = jax.random.normal(ks[3], (D_INNER, DT_RANK), dtype=jnp.float32) * s
            p[prefix + '_dt_b'] = jax.random.normal(ks[4], (D_INNER,), dtype=jnp.float32) * s
            p[prefix + '_Alog'] = jnp.log(jnp.broadcast_to(jnp.arange(1, D_STATE + 1, dtype=jnp.float32), (D_INNER, D_STATE)))
            p[prefix + '_D'] = jnp.ones((D_INNER,), dtype=jnp.float32)
            p[prefix + '_out_w'] = jax.random.normal(ks[5], (D_MODEL, D_INNER), dtype=jnp.float32) * s
            return p

        def _mamba(x, in_w, conv_w, conv_b, xproj_w, dt_w, dt_b, Alog, Dskip, out_w):
            B, L, _ = x.shape
            xz = jnp.einsum('bld,ed->ble', x, in_w)
            u, z = jnp.split(xz, 2, axis=-1)
            u_t = u.transpose(0, 2, 1)
            kern = conv_w[:, None, :]
            u_c = jax.lax.conv_general_dilated(u_t, kern, window_strides=(1,), padding=[(D_CONV - 1, 0)], feature_group_count=D_INNER)
            u = jax.nn.silu((u_c + conv_b[None, :, None]).transpose(0, 2, 1))
            x_dbl = jnp.einsum('bld,ed->ble', u, xproj_w)
            dt, Bm, Cm = jnp.split(x_dbl, [DT_RANK, DT_RANK + D_STATE], axis=-1)
            delta = jax.nn.softplus(jnp.einsum('blr,dr->bld', dt, dt_w) + dt_b)
            A = -jnp.exp(Alog)
            dA = jnp.exp(jnp.einsum('bld,dn->bldn', delta, A))
            dBu = jnp.einsum('bld,bln,bld->bldn', delta, Bm, u)

            def step(h, inp):
                dA_t, dBu_t, C_t = inp
                h = dA_t * h + dBu_t
                y = jnp.einsum('bdn,bn->bd', h, C_t)
                return (h, y)
            h0 = jnp.zeros((B, D_INNER, D_STATE), dtype=x.dtype)
            _, ys = jax.lax.scan(step, h0, (dA.transpose(1, 0, 2, 3), dBu.transpose(1, 0, 2, 3), Cm.transpose(1, 0, 2)))
            y = ys.transpose(1, 0, 2) + u * Dskip
            y = y * jax.nn.silu(z)
            return jnp.einsum('bld,od->blo', y, out_w)
        key = jax.random.key(seed)
        kx, kf, kb = jax.random.split(key, 3)
        inp = {'x': jax.random.normal(kx, (BATCH, SEQ, D_MODEL), dtype=jnp.float32)}
        inp.update(_init_params(kf, 'f'))
        inp.update(_init_params(kb, 'b'))
        return inp
    _L0_attn_all = _L0_attn_setup()
    _L0_attn_in = {k: v for k, v in _L0_attn_all.items() if k in ('f_in_w', 'f_conv_w', 'f_conv_b', 'f_xproj_w', 'f_dt_w', 'f_dt_b', 'f_Alog', 'f_D', 'f_out_w', 'b_in_w', 'b_conv_w', 'b_conv_b', 'b_xproj_w', 'b_dt_w', 'b_dt_b', 'b_Alog', 'b_D', 'b_out_w')}
    del _L0_attn_all

    def _L0_ffn_setup():
        import jax, jax.numpy as jnp
        import numpy as np
        E = 8
        K = 2
        D = 192
        F = 4 * D
        key = jax.random.key(seed)
        ks = jax.random.split(key, 10)
        s_exp = 0.02
        return {'x': jax.random.normal(ks[0], (4, 256, D), jnp.float32), 'W1': jax.random.normal(ks[1], (E, F, D), jnp.float32) * s_exp, 'b1': jax.random.normal(ks[2], (E, F), jnp.float32) * s_exp, 'W2': jax.random.normal(ks[3], (E, D, F), jnp.float32) * s_exp, 'b2': jax.random.normal(ks[4], (E, D), jnp.float32) * s_exp, 'Wr1': jax.random.normal(ks[5], (D, D), jnp.float32) * s_exp, 'br1': jax.random.normal(ks[6], (D,), jnp.float32) * s_exp, 'Wr2': jax.random.normal(ks[7], (E, D), jnp.float32) * s_exp, 'br2': jax.random.normal(ks[8], (E,), jnp.float32) * s_exp}
    _L0_ffn_all = _L0_ffn_setup()
    _L0_ffn_in = {k: v for k, v in _L0_ffn_all.items() if k in ('W1', 'b1', 'W2', 'b2', 'Wr1', 'br1', 'Wr2', 'br2')}
    del _L0_ffn_all
    return {'x': x, 'txt': txt, 'L0_tok_W_proj': _L0_tok_in['W_proj'], 'L0_tok_b_proj': _L0_tok_in['b_proj'], 'L0_tok_gamma': _L0_tok_in['gamma'], 'L0_tok_beta': _L0_tok_in['beta'], 'L0_attn_f_in_w': _L0_attn_in['f_in_w'], 'L0_attn_f_conv_w': _L0_attn_in['f_conv_w'], 'L0_attn_f_conv_b': _L0_attn_in['f_conv_b'], 'L0_attn_f_xproj_w': _L0_attn_in['f_xproj_w'], 'L0_attn_f_dt_w': _L0_attn_in['f_dt_w'], 'L0_attn_f_dt_b': _L0_attn_in['f_dt_b'], 'L0_attn_f_Alog': _L0_attn_in['f_Alog'], 'L0_attn_f_D': _L0_attn_in['f_D'], 'L0_attn_f_out_w': _L0_attn_in['f_out_w'], 'L0_attn_b_in_w': _L0_attn_in['b_in_w'], 'L0_attn_b_conv_w': _L0_attn_in['b_conv_w'], 'L0_attn_b_conv_b': _L0_attn_in['b_conv_b'], 'L0_attn_b_xproj_w': _L0_attn_in['b_xproj_w'], 'L0_attn_b_dt_w': _L0_attn_in['b_dt_w'], 'L0_attn_b_dt_b': _L0_attn_in['b_dt_b'], 'L0_attn_b_Alog': _L0_attn_in['b_Alog'], 'L0_attn_b_D': _L0_attn_in['b_D'], 'L0_attn_b_out_w': _L0_attn_in['b_out_w'], 'L0_ffn_W1': _L0_ffn_in['W1'], 'L0_ffn_b1': _L0_ffn_in['b1'], 'L0_ffn_W2': _L0_ffn_in['W2'], 'L0_ffn_b2': _L0_ffn_in['b2'], 'L0_ffn_Wr1': _L0_ffn_in['Wr1'], 'L0_ffn_br1': _L0_ffn_in['br1'], 'L0_ffn_Wr2': _L0_ffn_in['Wr2'], 'L0_ffn_br2': _L0_ffn_in['br2']}

def reference(x, txt, L0_tok_W_proj, L0_tok_b_proj, L0_tok_gamma, L0_tok_beta, L0_attn_f_in_w, L0_attn_f_conv_w, L0_attn_f_conv_b, L0_attn_f_xproj_w, L0_attn_f_dt_w, L0_attn_f_dt_b, L0_attn_f_Alog, L0_attn_f_D, L0_attn_f_out_w, L0_attn_b_in_w, L0_attn_b_conv_w, L0_attn_b_conv_b, L0_attn_b_xproj_w, L0_attn_b_dt_w, L0_attn_b_dt_b, L0_attn_b_Alog, L0_attn_b_D, L0_attn_b_out_w, L0_ffn_W1, L0_ffn_b1, L0_ffn_W2, L0_ffn_b2, L0_ffn_Wr1, L0_ffn_br1, L0_ffn_Wr2, L0_ffn_br2):
    import jax
    import jax.numpy as jnp

    def _L0_tok_ref(x, W_proj, b_proj, gamma, beta):
        import jax, jax.numpy as jnp
        import numpy as np
        P = 16
        EPS = 1e-05
        B, C, H, W = x.shape
        Hp, Wp = (H // P, W // P)
        patches = x.reshape(B, C, Hp, P, Wp, P)
        patches = patches.transpose(0, 2, 4, 1, 3, 5).reshape(B, Hp * Wp, C * P * P)
        y = jnp.einsum('bld,hd->blh', patches, W_proj) + b_proj
        mu = jnp.mean(y, axis=-1, keepdims=True)
        var = jnp.mean(jnp.square(y - mu), axis=-1, keepdims=True)
        y = (y - mu) * jax.lax.rsqrt(var + EPS) * gamma + beta
        return y

    def _L0_attn_ref(x, f_in_w, f_conv_w, f_conv_b, f_xproj_w, f_dt_w, f_dt_b, f_Alog, f_D, f_out_w, b_in_w, b_conv_w, b_conv_b, b_xproj_w, b_dt_w, b_dt_b, b_Alog, b_D, b_out_w):
        import jax, jax.numpy as jnp
        import numpy as np
        D_MODEL = 192
        D_STATE = 16
        EXPAND = 2
        D_INNER = EXPAND * D_MODEL
        DT_RANK = D_MODEL // 16
        D_CONV = 4
        BATCH = 2
        SEQ = 256

        def _init_params(key, prefix):
            ks = jax.random.split(key, 6)
            s = 0.02
            p = {}
            p[prefix + '_in_w'] = jax.random.normal(ks[0], (2 * D_INNER, D_MODEL), dtype=jnp.float32) * s
            p[prefix + '_conv_w'] = jax.random.normal(ks[1], (D_INNER, D_CONV), dtype=jnp.float32) * s
            p[prefix + '_conv_b'] = jnp.zeros((D_INNER,), dtype=jnp.float32)
            p[prefix + '_xproj_w'] = jax.random.normal(ks[2], (DT_RANK + 2 * D_STATE, D_INNER), dtype=jnp.float32) * s
            p[prefix + '_dt_w'] = jax.random.normal(ks[3], (D_INNER, DT_RANK), dtype=jnp.float32) * s
            p[prefix + '_dt_b'] = jax.random.normal(ks[4], (D_INNER,), dtype=jnp.float32) * s
            p[prefix + '_Alog'] = jnp.log(jnp.broadcast_to(jnp.arange(1, D_STATE + 1, dtype=jnp.float32), (D_INNER, D_STATE)))
            p[prefix + '_D'] = jnp.ones((D_INNER,), dtype=jnp.float32)
            p[prefix + '_out_w'] = jax.random.normal(ks[5], (D_MODEL, D_INNER), dtype=jnp.float32) * s
            return p

        def _mamba(x, in_w, conv_w, conv_b, xproj_w, dt_w, dt_b, Alog, Dskip, out_w):
            B, L, _ = x.shape
            xz = jnp.einsum('bld,ed->ble', x, in_w)
            u, z = jnp.split(xz, 2, axis=-1)
            u_t = u.transpose(0, 2, 1)
            kern = conv_w[:, None, :]
            u_c = jax.lax.conv_general_dilated(u_t, kern, window_strides=(1,), padding=[(D_CONV - 1, 0)], feature_group_count=D_INNER)
            u = jax.nn.silu((u_c + conv_b[None, :, None]).transpose(0, 2, 1))
            x_dbl = jnp.einsum('bld,ed->ble', u, xproj_w)
            dt, Bm, Cm = jnp.split(x_dbl, [DT_RANK, DT_RANK + D_STATE], axis=-1)
            delta = jax.nn.softplus(jnp.einsum('blr,dr->bld', dt, dt_w) + dt_b)
            A = -jnp.exp(Alog)
            dA = jnp.exp(jnp.einsum('bld,dn->bldn', delta, A))
            dBu = jnp.einsum('bld,bln,bld->bldn', delta, Bm, u)

            def step(h, inp):
                dA_t, dBu_t, C_t = inp
                h = dA_t * h + dBu_t
                y = jnp.einsum('bdn,bn->bd', h, C_t)
                return (h, y)
            h0 = jnp.zeros((B, D_INNER, D_STATE), dtype=x.dtype)
            _, ys = jax.lax.scan(step, h0, (dA.transpose(1, 0, 2, 3), dBu.transpose(1, 0, 2, 3), Cm.transpose(1, 0, 2)))
            y = ys.transpose(1, 0, 2) + u * Dskip
            y = y * jax.nn.silu(z)
            return jnp.einsum('bld,od->blo', y, out_w)
        fwd = _mamba(x, f_in_w, f_conv_w, f_conv_b, f_xproj_w, f_dt_w, f_dt_b, f_Alog, f_D, f_out_w)
        bwd = jnp.flip(_mamba(jnp.flip(x, 1), b_in_w, b_conv_w, b_conv_b, b_xproj_w, b_dt_w, b_dt_b, b_Alog, b_D, b_out_w), 1)
        return fwd + bwd

    def _L0_ffn_ref(x, W1, b1, W2, b2, Wr1, br1, Wr2, br2):
        import jax, jax.numpy as jnp
        import numpy as np
        E = 8
        K = 2
        D = 192
        F = 4 * D
        h = jax.nn.relu(jnp.einsum('bsd,hd->bsh', x, Wr1) + br1)
        score = jnp.einsum('bsd,ed->bse', h, Wr2) + br2
        _, idx = jax.lax.top_k(score, K)
        mask = (jax.nn.one_hot(idx, E) > 0).any(axis=-2)
        w = jax.nn.softmax(jnp.where(mask, score, -jnp.inf), axis=-1)
        out = jnp.zeros_like(x)
        for e in range(E):
            mid = jax.nn.relu(jnp.einsum('bsd,fd->bsf', x, W1[e]) + b1[e])
            ye = jnp.einsum('bsf,df->bsd', mid, W2[e]) + b2[e]
            out = out + w[..., e:e + 1] * ye
        return out
    h = _L0_tok_ref(x, L0_tok_W_proj, L0_tok_b_proj, L0_tok_gamma, L0_tok_beta)
    h = jnp.concatenate([h, txt], axis=1)
    h = h + _L0_attn_ref(_layernorm(h, axis=-1), L0_attn_f_in_w, L0_attn_f_conv_w, L0_attn_f_conv_b, L0_attn_f_xproj_w, L0_attn_f_dt_w, L0_attn_f_dt_b, L0_attn_f_Alog, L0_attn_f_D, L0_attn_f_out_w, L0_attn_b_in_w, L0_attn_b_conv_w, L0_attn_b_conv_b, L0_attn_b_xproj_w, L0_attn_b_dt_w, L0_attn_b_dt_b, L0_attn_b_Alog, L0_attn_b_D, L0_attn_b_out_w)
    h = h + _L0_ffn_ref(_layernorm(h, axis=-1), L0_ffn_W1, L0_ffn_b1, L0_ffn_W2, L0_ffn_b2, L0_ffn_Wr1, L0_ffn_br1, L0_ffn_Wr2, L0_ffn_br2)
    return h

_drawn_inputs = setup_inputs


def setup_inputs(seed=0):
    import zlib

    import numpy as np

    out = dict(_drawn_inputs(seed))
    spreads = {'L0_tok_gamma': (1.0, 0.2),
     'L0_tok_beta': (0.0, 0.1),
     'L0_attn_f_conv_b': (0.0, 0.8),
     'L0_attn_f_D': (1.0, 0.6),
     'L0_attn_b_conv_b': (0.0, 0.8),
     'L0_attn_b_D': (1.0, 0.6)}
    factors = {'L0_attn_f_in_w': 8.0,
     'L0_attn_f_conv_w': 8.0,
     'L0_attn_f_xproj_w': 8.0,
     'L0_attn_f_dt_w': 8.0,
     'L0_attn_f_dt_b': 8.0,
     'L0_attn_f_Alog': 8.0,
     'L0_attn_f_out_w': 8.0,
     'L0_attn_b_in_w': 8.0,
     'L0_attn_b_conv_w': 8.0,
     'L0_attn_b_xproj_w': 8.0,
     'L0_attn_b_dt_w': 8.0,
     'L0_attn_b_dt_b': 8.0,
     'L0_attn_b_Alog': 8.0,
     'L0_attn_b_out_w': 8.0,
     'L0_ffn_b1': 64.0,
     'L0_ffn_b2': 200.0,
     'L0_ffn_br1': 26.208,
     'L0_ffn_W1': 8.0,
     'L0_ffn_W2': 8.0,
     'L0_ffn_Wr1': 8.0,
     'L0_ffn_Wr2': 8.0,
     'L0_ffn_br2': 35.105}
    for name, (base, spread) in spreads.items():
        noise = np.random.default_rng([zlib.crc32(name.encode()), seed]).standard_normal(out[name].shape)
        drawn = base * np.exp(spread * noise) if base else spread * noise
        out[name] = jnp.asarray(drawn.astype(out[name].dtype))
    for name, factor in factors.items():
        out[name] = (out[name] * factor).astype(out[name].dtype)
    return out
```

```python
from contextlib import ExitStack

import numpy as np

import concourse.bass as bass
from concourse import mybir

F32 = mybir.dt.float32
ALU = mybir.AluOpType
ACT = mybir.ActivationFunctionType
AX = mybir.AxisListType

BATCH, IMG_TOK, TXT_TOK = 16, 64, 77
L = IMG_TOK + TXT_TOK
TOK = BATCH * L
D = 192
KD = D // 2
TP = 94
NT = TOK // TP
PATCH = 16
PK = 3 * PATCH * PATCH // 128
ET = BATCH * IMG_TOK // 128

DI = 2 * D
MD = DI // 128
NS = 16
RANK = D // 16
XP = RANK + 2 * NS
GB = 4
GT = GB * L
HG = GT // 2
NG = BATCH // GB
GTILES = GT // TP
CN = 4
NC = NS // CN
KI = NC * MD
CW = CN * GT
PADL = L + 6

NE = 8
FF = 4 * D
FM = FF // 128
EPS = 1e-5

POOL_STEPS = (0, 3, 6, 9)


def made_by(steps, it, k):
    return it * len(steps) + len([s for s in steps if s <= k])


VEC_STEPS = tuple(k for k in range(KI) if k not in POOL_STEPS)


def need(eng, sem, value):
    if not isinstance(value, int) or value > 0:
        eng.wait_ge(sem, value)


def fusion_kernel(nc, a, out):
    ctx = ExitStack()
    with ctx:
        def sb(name, shape, dt=F32):
            return ctx.enter_context(nc.sbuf_tensor(name, shape, dt))

        def sem(name):
            return ctx.enter_context(nc.semaphore(name))

        h = sb("h", [128, NT, D])
        xT = sb("xT", [128, 2, TOK])
        ident = sb("ident", [128, 128])
        stats = sb("stats", [128, NT, 6])
        mean = sb("mean", [128, NT])
        rstd = sb("rstd", [128, NT])
        lnt = sb("lnt", [128, 4, NT])
        in_w = sb("in_w", [128, 2, 2, 2 * DI])
        xp_w = sb("xp_w", [128, 2, MD, XP])
        dt_w = sb("dt_w", [128, 2, DI])
        out_w = sb("out_w", [128, 2, MD, D])
        conv_w = sb("conv_w", [128, 2, MD, 4])
        chan = sb("chan", [128, 2, 3, MD])
        negA = sb("negA", [128, 2, MD, NS])
        upad = sb("upad", [128, MD, GB, PADL])
        us = sb("us", [128, 2, MD, GT])
        sz = sb("sz", [128, 2, MD, GT])
        delta = sb("delta", [128, 2, MD, GT])
        du = sb("du", [128, 2, MD, GT])
        dbl = sb("dbl", [128, GT])
        bc = sb("bc", [128, 2, 2, CW])
        dA = sb("dA", [128, 2, CW])
        X = sb("X", [128, 3, CW])
        bcf = bc[:, :, :, :].rearrange("p a b n -> p (a b n)")
        Xf = X[:, :, :].rearrange("p a n -> p (a n)")
        dAf = dA[:, :, :].rearrange("p a n -> p (a n)")
        patches = bcf[:, 0:PK * 1024].rearrange("p (c n) -> p c n", c=PK)
        proj_w = bcf[:, PK * 1024:PK * 1024 + PK * D].rearrange("p (c n) -> p c n", c=PK)
        emb = Xf[:, 0:ET * D].rearrange("p (j d) -> p j d", j=ET)
        xn = Xf[:, ET * D:ET * D + 2 * 3 * D].rearrange("p (s j d) -> p s j d", s=2, j=3)
        embrow = dAf[:, 0:3 * D].rearrange("p (r d) -> p r d", r=3)
        w1 = bcf[:, 0:2 * 2 * FF].rearrange("p (s c f) -> p s c f", s=2, c=2)
        w2 = bcf[:, 4 * FF:4 * FF + 2 * FM * D].rearrange("p (s f d) -> p s f d", s=2, f=FM)
        mid = us[:, :, :, :].rearrange("p a m n -> p (a m n)").rearrange("p (s f n) -> p s f n", s=2, f=FM)
        szf = sz[:, :, :, :].rearrange("p a m n -> p (a m n)")
        hr = szf[:, 0:2 * 2 * HG].rearrange("p (s c n) -> p s c n", s=2, c=2)
        wr1 = szf[:, 1200:1200 + 2 * D].rearrange("p (c n) -> p c n", c=2)
        wr2 = szf[:, 1600:1600 + 2 * NE].rearrange("p (c n) -> p c n", c=2)
        br1 = szf[:, 1620:1622]
        br2 = szf[:, 1624:1624 + NE]
        b2 = szf[:, 1632:1632 + D]
        b1 = szf[:, 1824:1824 + NE * FM]
        dlf = delta[:, :, :, :].rearrange("p a m n -> p (a m n)")
        score, gate, rank, cmp_, gtop = (dlf[:, i * D:(i + 1) * D].rearrange("p (j e) -> p j e", e=NE) for i in range(5))
        rowmax, rowsum = dlf[:, 5 * D:5 * D + NT], dlf[:, 5 * D + NT:5 * D + 2 * NT]
        gateT = du[:, :, :, :].rearrange("p a m n -> p (a m n)")[:, 0:NT * TP].rearrange("p (j t) -> p j t", j=NT)

        pg = ctx.enter_context(nc.psum_tensor("pg", [128, 2, 2, 512], F32))
        py = ctx.enter_context(nc.psum_tensor("py", [128, 4, 512], F32))

        scratch = nc.dram_tensor("bc_rows", (2 * NG, 2 * NS, GT), F32, kind="Internal").ap()

        ld_patch, ld_emb, ld_txt, ld_w = sem("ld_patch"), sem("ld_emb"), sem("ld_txt"), sem("ld_w")
        emb_mm, emb_st, emb_dn, emb_h = sem("emb_mm"), sem("emb_st"), sem("emb_dn"), sem("emb_h")
        ln_chain, ln_sqrt, ln_in, ln_xn, ln_tr, ln_cp, ln_st = (
            sem("ln_chain"), sem("ln_sqrt"), sem("ln_in"), sem("ln_xn"), sem("ln_tr"), sem("ln_cp"), sem("ln_st"))
        passed = sem("passed")
        pads, aexp, aneg = sem("pads"), sem("aexp"), sem("aneg")
        u_mm, z_mm, xp_mm, dt_mm = sem("u_mm"), sem("z_mm"), sem("xp_mm"), sem("dt_mm")
        y_mm, op_mm = sem("y_mm"), sem("op_mm")
        u_cp, us_rdy, sz_rdy, dbl_rdy = sem("u_cp"), sem("us_rdy"), sem("sz_rdy"), sem("dbl_rdy")
        x_cp, abs_d, exp_d, sp_rdy, dA_rdy = sem("x_cp"), sem("abs_d"), sem("exp_d"), sem("sp_rdy"), sem("dA_rdy")
        tap_d, conv_d, relu_d = sem("tap_d"), sem("conv_d"), sem("relu_d")
        dbu_d, scan_d, hc_vec, y_part, y_fin, h_add = (
            sem("dbu_d"), sem("scan_d"), sem("hc_vec"), sem("y_part"), sem("y_fin"), sem("h_add"))
        zero_col = sem("zero_col")
        hc_pool, delta_d, du_d = sem("hc_pool"), sem("delta_d"), sem("du_d")
        bc_st = sem("bc_st")
        bc_ld = [sem("bc_ld0"), sem("bc_ld1")]
        ld_r, ld_e = sem("ld_r"), [sem("ld_e0"), sem("ld_e1")]
        r_mm, r_act, s_mm, s_cp, r_ch, r_exp, gt_tr, gt_cp, b2_mm = (
            sem("r_mm"), sem("r_act"), sem("s_mm"), sem("s_cp"), sem("r_ch"), sem("r_exp"), sem("gt_tr"),
            sem("gt_cp"), sem("b2_mm"))
        m_mm, m_act, e_mm, moe_add, stored = sem("m_mm"), sem("m_act"), sem("e_mm"), sem("moe_add"), sem("stored")

        block = ctx.enter_context(nc.Block())

        def apart(eng):
            eng.sem_inc(passed, 1)

        def y_pieces(m):
            q, left, t, found = m * GB, GB, 0, []
            while left:
                n = min(left, 3 - q % 3)
                found.append((q // 3, (q % 3) * L, t * L, n * L))
                q, left, t = q + n, left - n, t + n
            return found

        @block.sync
        def _(sp):
            sp.dma_start(patches, a["patches"].rearrange("(c p) n -> p c n", p=128)).then_inc(ld_patch, 16)
            sp.dma_start(proj_w, a["proj_wT"].rearrange("(c p) n -> p c n", p=128)).then_inc(ld_patch, 16)
            for r, name in enumerate(("proj_b", "gamma", "beta")):
                sp.dma_start(embrow[:, r, :], a[name].partition_broadcast(128)).then_inc(ld_emb, 16)
            for d, p in enumerate("fb"):
                sp.dma_start(in_w[0:KD, d], a[p + "_in_wT"].rearrange("(c p) n -> p c n", p=KD)).then_inc(ld_w, 16)
                sp.dma_start(xp_w[:, d], a[p + "_xproj_wT"].rearrange("(c p) n -> p c n", p=128)).then_inc(ld_w, 16)
                sp.dma_start(dt_w[0:RANK, d], a[p + "_dt_wT"]).then_inc(ld_w, 16)
                sp.dma_start(out_w[:, d], a[p + "_out_wT"].rearrange("(c p) n -> p c n", p=128)).then_inc(ld_w, 16)
                sp.dma_start(conv_w[:, d], a[p + "_conv_w"].rearrange("(m p) k -> p m k", p=128)).then_inc(ld_w, 16)
                sp.dma_start(negA[:, d], a[p + "_Alog"].rearrange("(m p) n -> p m n", p=128)).then_inc(ld_w, 16)
                sp.dma_start(chan[:, d], a[p + "_chan"]).then_inc(ld_w, 16)
            sp.wait_ge(emb_dn, 1)
            with nc.allow_non_contiguous_dma(reason="rows of 768 bytes"):
                sp.dma_start(h[0:64, 0::3, :], emb[0:64, :, :]).then_inc(emb_h, 16)
                sp.dma_start(h[47:94, 1::3, :], emb[64:111, :, :]).then_inc(emb_h, 16)
                sp.dma_start(h[0:17, 2::3, :], emb[111:128, :, :]).then_inc(emb_h, 16)

            def store_rows(g, d):
                it = 2 * g + d
                sp.wait_ge(dbl_rdy, it + 1)
                apart(sp)
                sp.dma_start(scratch[bass.ds(it, 1), :, :].rearrange("o n t -> (o n) t"),
                             dbl[RANK:XP, :]).then_inc(bc_st, 16)

            def load_chunk(g, d, c):
                it, s = 2 * g + d, c % 2
                need(sp, dbu_d, KI * it + MD * (c - 2) + MD)
                apart(sp)
                need(sp, hc_vec, made_by(VEC_STEPS, it, MD * (c - 2) + MD - 1) if c >= 2 else
                     made_by(VEC_STEPS, it - 1, MD * (c + 2) + MD - 1))
                apart(sp)
                need(sp, hc_pool, made_by(POOL_STEPS, it, MD * (c - 2) + MD - 1) if c >= 2 else
                     made_by(POOL_STEPS, it - 1, MD * (c + 2) + MD - 1))
                apart(sp)
                sp.wait_ge(bc_st, 16 * (it + 1))
                apart(sp)
                rows = scratch[bass.ds(it, 1), :, :].rearrange("o n t -> (o n) t")
                for w in range(2):
                    src = rows[w * NS + CN * c:w * NS + CN * (c + 1), :].rearrange("n t -> (n t)")
                    sp.dma_start(bc[:, s, w, :], src.partition_broadcast(128)).then_inc(bc_ld[s], 16)

            def group(g, last):
                for d in range(2):
                    for c in (2, 3):
                        load_chunk(g, d, c)
                    if d == 0 or not last:
                        n = (g, 1) if d == 0 else (g + 1, 0)
                        store_rows(*n)
                        load_chunk(*n, 0)
                        load_chunk(*n, 1)

            store_rows(0, 0)
            load_chunk(0, 0, 0)
            load_chunk(0, 0, 1)
            group(0, False)
            with sp.Fori(1, NG - 1) as g:
                group(g, False)
            group(NG - 1, True)

            sp.wait_ge(y_fin, 2 * NG * MD)
            sp.wait_ge(op_mm, 2 * 2 * NG)
            for dst, name in ((wr1[0:KD], "Wr1T"), (wr2[0:KD], "Wr2T")):
                sp.dma_start(dst, a[name].rearrange("(c p) n -> p c n", p=KD)).then_inc(ld_r, 16)
            with nc.allow_non_contiguous_dma(reason="small vectors"):
                sp.dma_start(br1[0:KD], a["br1"].rearrange("(c p) -> p c", p=KD)).then_inc(ld_r, 16)
                sp.dma_start(br2, a["br2"].partition_broadcast(128)).then_inc(ld_r, 16)
                sp.dma_start(b2[0:NE], a["b2"]).then_inc(ld_r, 16)
                sp.dma_start(b1, a["b1T"]).then_inc(ld_r, 16)

            def load_expert(e, s):
                sp.dma_start(w1[0:KD, s], a["W1T"][bass.ds(e, 1)].rearrange("o (c p) f -> p (o c) f", p=KD)).then_inc(ld_e[s], 16)
                sp.dma_start(w2[:, s], a["W2T"][bass.ds(e, 1)].rearrange("o (c p) f -> p (o c) f", p=128)).then_inc(ld_e[s], 16)

            load_expert(0, 0)
            load_expert(1, 1)
            with sp.Fori(1, NE // 2) as pair:
                for s in range(2):
                    sp.wait_ge(e_mm, 8 * (2 * pair + s - 1))
                    apart(sp)
                    load_expert(2 * pair + s, s)
            sp.wait_ge(moe_add, NT + 8 * NE)
            sp.dma_start(out.rearrange("b t d -> (b t) d").rearrange("(j p) d -> p j d", p=TP), h[0:TP]).then_inc(stored, 16)
            sp.wait_ge(stored, 16)

        @block.scalar
        def _(act):
            act.dma_start(ident[:, :], a["ident"]).then_inc(ld_txt, 16)
            txt = a["txt"]
            with nc.allow_non_contiguous_dma(reason="rows of 768 bytes"):
                act.dma_start(h[64:94, 0::3, :], txt[0::2, 0:30, :].rearrange("b t d -> t b d")).then_inc(ld_txt, 16)
                act.dma_start(h[0:47, 1::3, :], txt[0::2, 30:77, :].rearrange("b t d -> t b d")).then_inc(ld_txt, 16)
                act.dma_start(h[17:94, 2::3, :], txt[1::2, :, :].rearrange("b t d -> t b d")).then_inc(ld_txt, 16)
            act.wait_ge(ld_w, 16 * 14)
            nc.scalar.activation(negA[:, :, :, :], negA[:, :, :, :], ACT.Exp).then_inc(aexp, 1)

            def root(n, rows, count):
                act.wait_ge(ln_in, n)
                nc.scalar.activation(rstd[0:rows, 0:count], rstd[0:rows, 0:count], ACT.Sqrt).then_inc(ln_sqrt, 1)

            def copy_xT(base):
                with act.Fori(0, NG) as q2:
                    for s in range(2):
                        act.wait_ge(ln_tr, base + 2 * q2 + s + 1)
                        nc.scalar.activation(xT[0:KD, :, bass.ds(q2 * GT + s * HG, HG)],
                                             pg[0:KD, s, :, 0:HG], ACT.Copy).then_inc(ln_cp, 1)

            root(1, 128, ET)
            root(2, TP, NT)
            copy_xT(0)

            def copy_u(it):
                for m in range(MD):
                    act.wait_ge(u_mm, MD * it + m + 1)
                    need(act, conv_d, MD * (it - 1) + m + 1)
                    nc.scalar.activation(
                        upad[:, m, :, 3:3 + L].rearrange("p (a b) t -> p a b t", a=2),
                        pg[:, m % 2, :, 0:HG].rearrange("p a (b t) -> p a b t", b=2), ACT.Copy).then_inc(u_cp, 1)

            def silus(it, s):
                for m in range(MD):
                    act.wait_ge(conv_d, MD * it + m + 1)
                    nc.scalar.activation(us[:, s, m, :], us[:, s, m, :], ACT.Silu).then_inc(us_rdy, 1)
                for m in range(MD):
                    act.wait_ge(z_mm, MD * it + m + 1)
                    if m == 0:
                        need(act, y_fin, MD * (it - 1))
                    nc.scalar.activation(sz[:, s, m, :].rearrange("p (a n) -> p a n", a=2),
                                         pg[:, (m + 1) % 2, :, 0:HG], ACT.Silu).then_inc(sz_rdy, 1)

            def copy_dbl(it):
                act.wait_ge(xp_mm, it + 1)
                need(act, dt_mm, MD * it)
                need(act, bc_st, 16 * it)
                nc.scalar.activation(dbl[0:XP, :].rearrange("p (a n) -> p a n", a=2),
                                     pg[0:XP, 0, :, 0:HG], ACT.Copy).then_inc(dbl_rdy, 1)

            def softplus(it, s, d):
                for m in range(MD):
                    act.wait_ge(dt_mm, MD * it + m + 1)
                    if m == 0:
                        need(act, du_d, it - 1)
                        need(act, dA_rdy, KI * (it - 1))
                        need(act, dbu_d, KI * (it - 1))
                    nc.scalar.activation(du[:, s, m, :].rearrange("p (a n) -> p a n", a=2),
                                         pg[:, (m + 1) % 2, :, 0:HG], ACT.Identity, bias=chan[:, d, 1, m:m + 1]).then_inc(x_cp, 1)
                act.wait_ge(x_cp, MD * (it + 1))
                nc.scalar.activation(delta[:, s], du[:, s], ACT.Abs).then_inc(abs_d, 1)
                act.wait_ge(abs_d, it + 1)
                nc.scalar.activation(delta[:, s], delta[:, s], ACT.Exp, scale=-1.0).then_inc(exp_d, 1)
                act.wait_ge(exp_d, it + 1)
                nc.scalar.activation(delta[:, s], delta[:, s], ACT.Ln, bias=1.0).then_inc(sp_rdy, 1)

            def decay(it, s, d, k):
                c, m = k // MD, k % MD
                if k == 0:
                    act.wait_ge(delta_d, it + 1)
                need(act, scan_d, KI * it + k - 1)
                rows = dA[:, k % 2, :].rearrange("p (n b t) -> p n b t", n=CN, b=GB)
                src = delta[:, s, m, :].rearrange("p (b t) -> p b t", b=GB)
                t0, t1 = (1, L) if d == 0 else (0, L - 1)
                for n in range(CN):
                    last = nc.scalar.activation(rows[:, n, :, t0:t1], src[:, :, t0:t1], ACT.Exp,
                                                scale=negA[:, d, m, CN * c + n:CN * c + n + 1])
                last.then_inc(dA_rdy, 1)

            def group(g, last):
                for d in range(2):
                    it = 2 * g + d
                    more = d == 0 or not last
                    for k in range(KI):
                        decay(it, d, d, k)
                        if more and k == 2:
                            copy_u(it + 1)
                        if more and k == 5:
                            silus(it + 1, 1 - d)
                        if more and k == 7:
                            copy_dbl(it + 1)
                        if more and k == 9:
                            softplus(it + 1, 1 - d, 1 - d)

            act.wait_ge(aneg, 1)
            copy_u(0)
            silus(0, 0)
            copy_dbl(0)
            softplus(0, 0, 0)
            group(0, False)
            with act.Fori(1, NG - 1) as g:
                group(g, False)
            group(NG - 1, True)

            root(3, TP, NT)
            copy_xT(8)
            act.wait_ge(ld_r, 16 * 6)
            with act.Fori(0, NG) as q2:
                for s in range(2):
                    act.wait_ge(r_mm, 2 * q2 + s + 1)
                    for c in range(2):
                        last = nc.scalar.activation(hr[0:KD, s, c, :], pg[0:KD, s, c, 0:HG], ACT.Relu, bias=br1[0:KD, c:c + 1])
                    last.then_inc(r_act, 1)
            act.wait_ge(r_ch, 1)
            nc.scalar.activation(gate[0:TP], gtop[0:TP], ACT.Exp).then_inc(r_exp, 1)
            with act.Fori(0, NE) as e:
                with act.Fori(0, NG) as q2:
                    for s in range(2):
                        for f in range(FM):
                            j = FM * s + f
                            act.wait_ge(m_mm, 48 * e + 12 * q2 + j + 1)
                            apart(act)
                            nc.scalar.activation(mid[:, s, f, :], pg[:, j % 4 // 2, j % 2, 0:HG], ACT.Relu,
                                                 bias=b1[:, bass.ds(FM * e + f, 1)]).then_inc(m_act, 1)

        @block.tensor
        def _(pe):
            pe.wait_ge(ld_patch, 32)
            for j in range(ET):
                need(pe, emb_st, j - 1)
                for c in range(PK):
                    last = nc.tensor.matmul(pg[:, j % 2, 0, 0:D], patches[:, c, 128 * j:128 * (j + 1)], proj_w[:, c, :],
                                            start=(c == 0), stop=(c == PK - 1))
                last.then_inc(emb_mm, 1)

            def transposes(base):
                with pe.Fori(0, NG) as q2:
                    for s in range(2):
                        pe.wait_ge(ln_xn, base + 2 * q2 + s + 1)
                        for c in range(2):
                            for j in range(3):
                                last = nc.tensor.transpose(pg[0:KD, s, c, TP * j:TP * (j + 1)],
                                                           xn[0:TP, s, j, KD * c:KD * (c + 1)], ident[0:TP, 0:TP])
                        last.then_inc(ln_tr, 1)

            pe.wait_ge(ld_txt, 64)
            pe.wait_ge(emb_st, ET)
            transposes(0)
            pe.wait_ge(ln_cp, 8)
            pe.wait_ge(ld_w, 16 * 14)

            def in_proj(g, d, m, slot):
                apart(pe)
                for half in range(2):
                    for c in range(2):
                        last = nc.tensor.matmul(pg[:, slot, half, 0:HG], in_w[0:KD, d, c, 128 * m:128 * (m + 1)],
                                                xT[0:KD, c, bass.ds(g * GT + half * HG, HG)],
                                                start=(c == 0), stop=(c == 1))
                return last

            def proj_u(g, d, m):
                it = 2 * g + d
                if m == 0:
                    need(pe, x_cp, MD * (it - 1) + 2)
                if m == 1:
                    need(pe, x_cp, MD * it)
                if m == 2:
                    pe.wait_ge(u_cp, MD * it + 1)
                in_proj(g, d, m, m % 2).then_inc(u_mm, 1)

            def proj_z(g, d, m):
                it = 2 * g + d
                if m == 0:
                    pe.wait_ge(u_cp, MD * it + 2)
                    need(pe, h_add, 2 * (it - 1) - 1)
                if m == 1:
                    pe.wait_ge(u_cp, MD * it + 3)
                    need(pe, h_add, 2 * (it - 1))
                if m == 2:
                    pe.wait_ge(sz_rdy, MD * it + 1)
                in_proj(g, d, MD + m, (m + 1) % 2).then_inc(z_mm, 1)

            def xproj(g, d):
                it = 2 * g + d
                pe.wait_ge(us_rdy, MD * (it + 1))
                pe.wait_ge(sz_rdy, MD * it + 2)
                for half in range(2):
                    for m in range(MD):
                        last = nc.tensor.matmul(pg[0:XP, 0, half, 0:HG], xp_w[:, d, m, :],
                                                us[:, d, m, half * HG:(half + 1) * HG],
                                                start=(m == 0), stop=(m == MD - 1))
                last.then_inc(xp_mm, 1)

            def dt_proj(g, d, m):
                it = 2 * g + d
                if m == 0:
                    pe.wait_ge(dbl_rdy, it + 1)
                    pe.wait_ge(sz_rdy, MD * it + 3)
                if m == 2:
                    pe.wait_ge(x_cp, MD * it + 1)
                for half in range(2):
                    last = nc.tensor.matmul(pg[:, (m + 1) % 2, half, 0:HG], dt_w[0:RANK, d, 128 * m:128 * (m + 1)],
                                            dbl[0:RANK, half * HG:(half + 1) * HG], start=True, stop=True)
                last.then_inc(dt_mm, 1)

            def out_proj(it, d, part):
                tiles = (range(0, 4), range(4, GTILES))[part]
                if part == 0:
                    pe.wait_ge(y_fin, MD * (it + 1))
                for j in tiles:
                    o = j - tiles[0]
                    for m in range(MD):
                        last = nc.tensor.matmul(pg[0:TP, 1 - part, o // 2, D * (o % 2):D * (o % 2) + D],
                                                us[:, d, m, TP * j:TP * (j + 1)], out_w[:, d, m, :],
                                                start=(m == 0), stop=(m == MD - 1))
                last.then_inc(op_mm, 1)

            def sum_states(it, d, k):
                c, m = k // MD, k % MD
                if c == 0:
                    need(pe, y_part, 6 * (it - 1) + (3, 5, 6)[m])
                if k in POOL_STEPS:
                    pe.wait_ge(hc_pool, made_by(POOL_STEPS, it, k))
                else:
                    pe.wait_ge(hc_vec, made_by(VEC_STEPS, it, k))
                first_in_bank = {0: (True, True), 1: (False, True), 2: (False, True)}[m]
                for n in range(CN):
                    for (bank, col, tok, w), fresh in zip(y_pieces(m), first_in_bank):
                        last = nc.tensor.matmul(py[:, bank, col:col + w], ident[:, :],
                                                X[:, k % 3, n * GT + tok:n * GT + tok + w],
                                                start=(fresh and c == 0 and n == 0), stop=(c == NC - 1 and n == CN - 1),
                                                skip_group_check=True)
                last.then_inc(y_mm, 1)

            def group(g, first, last):
                for d in range(2):
                    it = 2 * g + d
                    more = d == 0 or not last
                    prev = d == 1 or not first
                    n = (g, 1) if d == 0 else (g + 1, 0)
                    for k in range(KI):
                        if more:
                            if k == 0:
                                proj_u(*n, 0)
                                proj_u(*n, 1)
                            if k == 3:
                                proj_u(*n, 2)
                        if prev and k == 3:
                            if more:
                                pe.wait_ge(u_cp, MD * (it + 1) + 2)
                            else:
                                pe.wait_ge(x_cp, MD * (it + 1))
                            out_proj(it - 1, 1 - d, 0)
                        if prev and k == 4:
                            if more:
                                pe.wait_ge(u_cp, MD * (it + 1) + 3)
                            out_proj(it - 1, 1 - d, 1)
                        if more:
                            if k == 5:
                                proj_z(*n, 0)
                                proj_z(*n, 1)
                            if k == 6:
                                proj_z(*n, 2)
                            if k == 7:
                                xproj(*n)
                            if k == 9:
                                dt_proj(*n, 0)
                                dt_proj(*n, 1)
                            if k == 10:
                                dt_proj(*n, 2)
                        sum_states(it, d, k)

            for m in range(MD):
                proj_u(0, 0, m)
            for m in range(MD):
                proj_z(0, 0, m)
            xproj(0, 0)
            for m in range(MD):
                dt_proj(0, 0, m)
            group(0, True, False)
            with pe.Fori(1, NG - 1) as g:
                group(g, False, False)
            group(NG - 1, False, True)
            pe.wait_ge(h_add, 2 * (2 * NG - 1))
            out_proj(2 * NG - 1, 1, 0)
            out_proj(2 * NG - 1, 1, 1)

            pe.wait_ge(h_add, 4 * NG)
            transposes(8)
            pe.wait_ge(ln_cp, 16)
            pe.wait_ge(ld_r, 16 * 6)
            pe.wait_ge(y_part, 12 * NG)
            with pe.Fori(0, NG) as q2:
                for s in range(2):
                    for c in range(2):
                        for k in range(2):
                            last = nc.tensor.matmul(pg[0:KD, s, c, 0:HG], wr1[0:KD, k, KD * c:KD * (c + 1)],
                                                    xT[0:KD, k, bass.ds(q2 * GT + s * HG, HG)], start=(k == 0), stop=(k == 1))
                    last.then_inc(r_mm, 1)
                for s in range(2):
                    pe.wait_ge(r_act, 2 * q2 + s + 1)
                    for j in range(3):
                        for c in range(2):
                            last = nc.tensor.matmul(py[0:TP, s, NE * j:NE * (j + 1)], hr[0:KD, s, c, TP * j:TP * (j + 1)],
                                                    wr2[0:KD, c, :], start=(c == 0), stop=(c == 1))
                    last.then_inc(s_mm, 1)
                pe.wait_ge(s_cp, 2 * q2 + 2)
            pe.wait_ge(r_ch, 2)
            for j in range(NT):
                last = nc.tensor.transpose(pg[0:NE, j // 5 // 2 % 2, j // 5 % 2, TP * (j % 5):TP * (j % 5 + 1)] if j < 20 else
                                           py[0:NE, 0, TP * (j - 20):TP * (j - 19)], gate[0:TP, j, :], ident[0:TP, 0:TP])
            last.then_inc(gt_tr, 1)
            pe.wait_ge(gt_cp, 1)
            for j in range(NT):
                need(pe, moe_add, j - 3)
                nc.tensor.matmul(py[0:TP, j % 4, 0:D], gateT[0:NE, j, :], b2[0:NE, :], start=True, stop=True).then_inc(b2_mm, 1)
            pe.wait_ge(moe_add, NT)

            def expert(pair, s_e):
                e = 2 * pair + s_e
                pe.wait_ge(ld_e[s_e], 32 * (pair + 1))
                apart(pe)
                with pe.Fori(0, NG) as q2:
                    for s in range(2):
                        for f in range(FM):
                            j = FM * s + f
                            if f >= 4:
                                pe.wait_ge(m_act, 48 * e + 12 * q2 + j - 3)
                                apart(pe)
                            for c in range(2):
                                last = nc.tensor.matmul(pg[:, j % 4 // 2, j % 2, 0:HG], w1[0:KD, s_e, c, 128 * f:128 * (f + 1)],
                                                        xT[0:KD, c, bass.ds(q2 * GT + s * HG, HG)], start=(c == 0), stop=(c == 1))
                            last.then_inc(m_mm, 1)
                        pe.wait_ge(m_act, 48 * e + 12 * q2 + FM * s + FM)
                        pe.wait_ge(moe_add, NT + 8 * e + 2 * q2 + s - 1)
                        for j in range(3):
                            for f in range(FM):
                                last = nc.tensor.matmul(py[0:TP, 2 * s + j // 2, D * (j % 2):D * (j % 2) + D],
                                                        mid[:, s, f, TP * j:TP * (j + 1)], w2[:, s_e, f, :],
                                                        start=(f == 0), stop=(f == FM - 1))
                        last.then_inc(e_mm, 1)

            with pe.Fori(0, NE // 2) as pair:
                for s_e in range(2):
                    expert(pair, s_e)

        @block.vector
        def _(dve):
            chain = [0]

            def then_next(ins):
                chain[0] += 1
                ins.then_inc(ln_chain, 1)
                dve.wait_ge(ln_chain, chain[0])

            nc.vector.memset(upad[:, :, :, :], 0.0).then_inc(pads, 1)
            dve.wait_ge(pads, 1)
            dve.wait_ge(aexp, 1)
            nc.vector.tensor_scalar(negA[:, :, :, :], negA[:, :, :, :], -1.0, None, ALU.mult).then_inc(aneg, 1)

            def moments(n, rows, count):
                st = stats[0:rows, 0:count, :]
                s0, s1, s2 = (lnt[0:rows, i, 0:count] for i in range(3))
                then_next(nc.vector.tensor_tensor(s0, st[:, :, 1], st[:, :, 4], ALU.add))
                then_next(nc.vector.tensor_tensor(s1, st[:, :, 1], st[:, :, 4], ALU.subtract))
                then_next(nc.vector.tensor_tensor(s2, st[:, :, 2], st[:, :, 5], ALU.add))
                then_next(nc.vector.tensor_scalar(mean[0:rows, 0:count], s0, 0.5, None, ALU.mult))
                then_next(nc.vector.scalar_tensor_tensor(s1, s1, 0.25, s1, ALU.mult, ALU.mult))
                then_next(nc.vector.scalar_tensor_tensor(s2, s2, 1.0 / D, s1, ALU.mult, ALU.add))
                nc.vector.tensor_scalar(rstd[0:rows, 0:count], s2, EPS, None, ALU.add).then_inc(ln_in, 1)
                dve.wait_ge(ln_sqrt, n)
                then_next(nc.vector.reciprocal(rstd[0:rows, 0:count], rstd[0:rows, 0:count]))

            dve.wait_ge(ld_emb, 48)
            for j in range(ET):
                dve.wait_ge(emb_mm, j + 1)
                nc.vector.tensor_tensor(emb[:, j, :], pg[:, j % 2, 0, 0:D], embrow[:, 0, :], ALU.add).then_inc(emb_st, 1)
                dve.wait_ge(emb_st, j + 1)
                then_next(nc.vector.bn_stats(stats[:, j, :], emb[:, j, :]))
            moments(1, 128, ET)
            for j in range(ET):
                last = nc.vector.tensor_scalar(emb[:, j, :], emb[:, j, :], mean[:, j:j + 1], rstd[:, j:j + 1],
                                               ALU.subtract, ALU.mult)
            then_next(last)
            row = lambda r: embrow[:, r, :].unsqueeze(1).to_broadcast([128, ET, D])
            then_next(nc.vector.tensor_tensor(emb, emb, row(1), ALU.mult))
            nc.vector.tensor_tensor(emb, emb, row(2), ALU.add).then_inc(emb_dn, 1)

            def normalise(n, base):
                with dve.Fori(0, NT) as j:
                    last = nc.vector.bn_stats(stats[0:TP, bass.ds(j, 1), :].rearrange("p o s -> p (o s)"),
                                              h[0:TP, bass.ds(j, 1), :].rearrange("p o d -> p (o d)")).then_inc(ln_st, 1)
                dve.wait_ge(ln_st, NT * (n - 1))
                moments(n, TP, NT)
                with dve.Fori(0, NG) as q2:
                    for s in range(2):
                        for j in range(3):
                            t = 6 * q2 + 3 * s + j
                            last = nc.vector.tensor_scalar(xn[0:TP, s, j, :], h[0:TP, bass.ds(t, 1), :].rearrange("p o d -> p (o d)"),
                                                           mean[0:TP, bass.ds(t, 1)], rstd[0:TP, bass.ds(t, 1)],
                                                           ALU.subtract, ALU.mult)
                        last.then_inc(ln_xn, 1)
                    dve.wait_ge(ln_cp, base + 2 * q2 + 2)

            dve.wait_ge(ld_txt, 64)
            dve.wait_ge(emb_h, 48)
            normalise(2, 0)

            def conv(it, s, d):
                need(dve, op_mm, 2 * (it - 1))
                for m in range(MD):
                    dve.wait_ge(u_cp, MD * it + m + 1)
                    dst = us[:, s, m, :].rearrange("p (b t) -> p b t", b=GB)
                    for k in range(4):
                        o = k if d == 0 else 6 - k
                        src = upad[:, m, :, o:o + L]
                        w = conv_w[:, d, m, k:k + 1]
                        if k == 0:
                            nc.vector.tensor_scalar(dst, src, w, chan[:, d, 0, m:m + 1], ALU.mult, ALU.add).then_inc(tap_d, 1)
                        else:
                            dve.wait_ge(tap_d, 3 * MD * it + 3 * m + k)
                            nc.vector.scalar_tensor_tensor(dst, src, w, dst, ALU.mult, ALU.add)\
                                .then_inc(conv_d if k == 3 else tap_d, 1)

            def relu(it, s):
                dve.wait_ge(abs_d, it + 1)
                nc.vector.tensor_scalar(du[:, s], du[:, s], 0.0, None, ALU.max).then_inc(relu_d, 1)

            def scan_step(it, s, d, k):
                c, m = k // MD, k % MD
                x = X[:, k % 3, :]
                xs = x.rearrange("p (n t) -> p n t", n=CN)
                if k == 0:
                    dve.wait_ge(du_d, it + 1)
                if m == 0:
                    dve.wait_ge(bc_ld[c % 2], 64 * it + 32 * (c // 2) + 32)
                need(dve, y_mm, KI * it + k - 2)
                nc.vector.tensor_tensor(xs, du[:, s, m, :].unsqueeze(1).to_broadcast([128, CN, GT]),
                                        bc[:, c % 2, 0, :].rearrange("p (n t) -> p n t", n=CN), ALU.mult).then_inc(dbu_d, 1)
                if k < 2:
                    t0 = 0 if d == 0 else L - 1
                    need(dve, scan_d, KI * it + k - 1)
                    nc.vector.memset(dA[:, k % 2, :].rearrange("p (r t) -> p r t", t=L)[:, :, t0:t0 + 1], 0.0).then_inc(zero_col, 1)
                    dve.wait_ge(zero_col, 2 * it + k + 1)
                dve.wait_ge(dA_rdy, KI * it + k + 1)
                dve.wait_ge(dbu_d, KI * it + k + 1)
                dec = dA[:, k % 2, :]
                if d == 1:
                    x, dec = x[:, ::-1], dec[:, ::-1]
                nc.vector.tensor_tensor_scan(x, dec, x, 0.0, ALU.mult, ALU.add).then_inc(scan_d, 1)
                if k in VEC_STEPS:
                    dve.wait_ge(scan_d, KI * it + k + 1)
                    nc.vector.tensor_tensor(xs, xs, bc[:, c % 2, 1, :].rearrange("p (n t) -> p n t", n=CN), ALU.mult).then_inc(hc_vec, 1)

            def finish(it, s, d):
                dve.wait_ge(y_mm, KI * (it + 1))
                for m in range(MD):
                    for bank, col, tok, w in y_pieces(m):
                        dst = us[:, s, m, tok:tok + w]
                        nc.vector.scalar_tensor_tensor(dst, dst, chan[:, d, 2, m:m + 1], py[:, bank, col:col + w],
                                                       ALU.mult, ALU.add).then_inc(y_part, 1)
                    dve.wait_ge(y_part, 6 * it + 2 * m + 2)
                    nc.vector.tensor_tensor(us[:, s, m, :], us[:, s, m, :], sz[:, s, m, :], ALU.mult).then_inc(y_fin, 1)

            def add_out(g, it, part):
                tiles = (range(0, 4), range(4, GTILES))[part]
                n = len(tiles) // 2
                dve.wait_ge(op_mm, 2 * it + part + 1)
                need(dve, h_add, 2 * it + part)
                dst = h[0:TP, bass.ds(GTILES * g + tiles[0], 2 * n), :].rearrange("p (a b) d -> p a b d", a=n)
                nc.vector.tensor_tensor(dst, dst, pg[0:TP, 1 - part, 0:n, 0:2 * D].rearrange("p a (b d) -> p a b d", b=2),
                                        ALU.add).then_inc(h_add, 1)

            def group(g, first, last):
                for d in range(2):
                    it = 2 * g + d
                    more = d == 0 or not last
                    prev = d == 1 or not first
                    for k in range(KI):
                        if prev and k == 1:
                            finish(it - 1, 1 - d, 1 - d)
                        if prev and k == 5:
                            add_out(g - 1 if d == 0 else g, it - 1, 0)
                            add_out(g - 1 if d == 0 else g, it - 1, 1)
                        if more and k == 4:
                            conv(it + 1, 1 - d, 1 - d)
                        if more and k == 11:
                            relu(it + 1, 1 - d)
                        scan_step(it, d, d, k)

            dve.wait_ge(ld_w, 16 * 14)
            conv(0, 0, 0)
            relu(0, 0)
            group(0, True, False)
            with dve.Fori(1, NG - 1) as g:
                group(g, False, False)
            group(NG - 1, False, True)
            finish(2 * NG - 1, 1, 1)
            add_out(NG - 1, 2 * NG - 1, 0)
            add_out(NG - 1, 2 * NG - 1, 1)
            dve.wait_ge(h_add, 4 * NG)

            normalise(3, 8)
            dve.wait_ge(ld_r, 16 * 6)
            with dve.Fori(0, NG) as q2:
                for s in range(2):
                    dve.wait_ge(s_mm, 2 * q2 + s + 1)
                    nc.vector.tensor_tensor(score[0:TP, bass.ds(6 * q2 + 3 * s, 3), :],
                                            py[0:TP, s, 0:3 * NE].rearrange("p (j e) -> p j e", j=3),
                                            br2[0:TP, :].unsqueeze(1).to_broadcast([TP, 3, NE]), ALU.add).then_inc(s_cp, 1)
            dve.wait_ge(s_cp, 8)
            sc, rk, cm = score[0:TP], rank[0:TP], cmp_[0:TP]
            then_next(nc.vector.memset(rk, 0.0))
            for o in range(NE):
                other = score[0:TP, :, o:o + 1]
                then_next(nc.vector.tensor_tensor(cm[:, :, 0:o + 1], other.to_broadcast([TP, NT, o + 1]), sc[:, :, 0:o + 1], ALU.is_gt))
                if o < NE - 1:
                    then_next(nc.vector.tensor_tensor(cm[:, :, o + 1:NE], other.to_broadcast([TP, NT, NE - 1 - o]), sc[:, :, o + 1:NE], ALU.is_ge))
                then_next(nc.vector.tensor_tensor(rk, rk, cm, ALU.add))
            then_next(nc.vector.tensor_scalar(rk, rk, 1.5, None, ALU.is_lt))
            then_next(nc.vector.tensor_reduce(rowmax[0:TP], sc, AX.X, ALU.max))
            nc.vector.tensor_tensor(gtop[0:TP], sc, rowmax[0:TP].unsqueeze(2).to_broadcast([TP, NT, NE]), ALU.subtract).then_inc(r_ch, 1)
            dve.wait_ge(r_exp, 1)
            then_next(nc.vector.tensor_tensor(gate[0:TP], gate[0:TP], rk, ALU.mult))
            then_next(nc.vector.tensor_reduce(rowsum[0:TP], gate[0:TP], AX.X, ALU.add))
            then_next(nc.vector.reciprocal(rowsum[0:TP], rowsum[0:TP]))
            nc.vector.tensor_tensor(gate[0:TP], gate[0:TP], rowsum[0:TP].unsqueeze(2).to_broadcast([TP, NT, NE]), ALU.mult).then_inc(r_ch, 1)
            dve.wait_ge(gt_tr, 1)
            for b in range(5):
                w = min(5, NT - 5 * b) * TP
                src = pg[0:NE, b // 2, b % 2, 0:w] if b < 4 else py[0:NE, 0, 0:w]
                last = nc.vector.tensor_copy(gateT[0:NE, 5 * b:5 * b + w // TP, :].rearrange("p j t -> p (j t)"), src)
            last.then_inc(gt_cp, 1)
            for j in range(NT):
                dve.wait_ge(b2_mm, j + 1)
                nc.vector.tensor_tensor(h[0:TP, j, :], h[0:TP, j, :], py[0:TP, j % 4, 0:D], ALU.add).then_inc(moe_add, 1)
            dve.wait_ge(moe_add, NT)
            dve.wait_ge(r_ch, 2)

            with dve.Fori(0, NE) as e:
                with dve.Fori(0, NG) as q2:
                    for s in range(2):
                        dve.wait_ge(e_mm, 8 * e + 2 * q2 + s + 1)
                        dve.wait_ge(moe_add, NT - 7 + 8 * e + 2 * q2 + s)
                        for j in range(3):
                            t = 6 * q2 + 3 * s + j
                            hh = h[0:TP, bass.ds(t, 1), :].rearrange("p o d -> p (o d)")
                            last = nc.vector.scalar_tensor_tensor(
                                hh, py[0:TP, 2 * s + j // 2, D * (j % 2):D * (j % 2) + D],
                                dlf[0:TP, bass.ds(D + t * NE + e, 1)], hh, ALU.mult, ALU.add)
                        last.then_inc(moe_add, 1)

        @block.gpsimd
        def _(pool):
            def softplus_sum(it, s):
                pool.wait_ge(sp_rdy, it + 1)
                pool.wait_ge(relu_d, it + 1)
                nc.gpsimd.tensor_tensor(delta[:, s], delta[:, s], du[:, s], ALU.add).then_inc(delta_d, 1)
                pool.wait_ge(delta_d, it + 1)
                pool.wait_ge(us_rdy, MD * (it + 1))
                nc.gpsimd.tensor_tensor(du[:, s], delta[:, s], us[:, s], ALU.mult).then_inc(du_d, 1)

            def group(g, last):
                for d in range(2):
                    it = 2 * g + d
                    for k in POOL_STEPS:
                        c = k // MD
                        pool.wait_ge(scan_d, KI * it + k + 1)
                        x = X[:, k % 3, :]
                        pool.wait_ge(bc_ld[c % 2], 64 * it + 32 * (c // 2) + 32)
                        nc.gpsimd.tensor_tensor(x, x, bc[:, c % 2, 1, :], ALU.mult).then_inc(hc_pool, 1)
                    if d == 0 or not last:
                        softplus_sum(it + 1, 1 - d)

            softplus_sum(0, 0)
            group(0, False)
            with pool.Fori(1, NG - 1) as g:
                group(g, False)
            group(NG - 1, True)


def kernel(**inputs):
    import concourse.bacc as bacc
    from concourse.bass_utils import run_bass_kernel_spmd

    v = {n: np.asarray(x) for n, x in inputs.items()}
    P = PATCH
    x = v["x"]
    hp, wp = x.shape[2] // P, x.shape[3] // P
    host = {
        "patches": x.reshape(BATCH, 3, hp, P, wp, P).transpose(1, 3, 5, 0, 2, 4).reshape(3 * P * P, BATCH * hp * wp),
        "txt": v["txt"], "proj_wT": v["L0_tok_W_proj"].T, "proj_b": v["L0_tok_b_proj"],
        "gamma": v["L0_tok_gamma"], "beta": v["L0_tok_beta"],
        "W1T": v["L0_ffn_W1"].transpose(0, 2, 1), "W2T": v["L0_ffn_W2"].transpose(0, 2, 1),
        "b1T": v["L0_ffn_b1"].reshape(NE, FM, 128).transpose(2, 0, 1).reshape(128, NE * FM),
        "b2": v["L0_ffn_b2"], "Wr1T": v["L0_ffn_Wr1"].T, "br1": v["L0_ffn_br1"],
        "Wr2T": v["L0_ffn_Wr2"].T, "br2": v["L0_ffn_br2"], "ident": np.eye(128, dtype=np.float32),
    }
    for p in "fb":
        w = {n: v[f"L0_attn_{p}_{n}"] for n in ("in_w", "conv_w", "conv_b", "xproj_w", "dt_w", "dt_b", "Alog", "D", "out_w")}
        host.update({p + "_in_wT": w["in_w"].T, p + "_xproj_wT": w["xproj_w"].T, p + "_dt_wT": w["dt_w"].T,
                     p + "_out_wT": w["out_w"].T, p + "_conv_w": w["conv_w"], p + "_Alog": w["Alog"],
                     p + "_chan": np.stack([w[n].reshape(MD, 128).T for n in ("conv_b", "dt_b", "D")], axis=1)})
    nc = bacc.Bacc("TRN2", target_bir_lowering=False, num_devices=1)
    arrays, aps = {}, {}
    for n, arr in host.items():
        arrays["in_" + n] = np.ascontiguousarray(arr)
        aps[n] = nc.dram_tensor("in_" + n, arrays["in_" + n].shape, F32, kind="ExternalInput").ap()
    out = nc.dram_tensor("out_0", (BATCH, L, D), F32, kind="ExternalOutput").ap()
    fusion_kernel(nc, aps, out)
    r = run_bass_kernel_spmd(nc, [arrays], core_ids=[0])
    return r.results[0]["out_0"]
```

```python
from contextlib import ExitStack

import numpy as np

import concourse.bass as bass
from concourse import mybir

F32 = mybir.dt.float32
I32 = mybir.dt.int32
U32 = mybir.dt.uint32
ALU = mybir.AluOpType
ACT = mybir.ActivationFunctionType
AX = mybir.AxisListType

BATCH, IMG_TOK, TXT_TOK = 16, 64, 77
L = IMG_TOK + TXT_TOK
TOK = BATCH * L
D = 192
KD = D // 2
TP = 94
NT = TOK // TP
PATCH = 16
PK = 3 * PATCH * PATCH // 128
ET = BATCH * IMG_TOK // 128

DI = 2 * D
MD = DI // 128
NS = 16
RANK = D // 16
XP = RANK + 2 * NS
GB = 4
GT = GB * L
HG = GT // 2
NG = BATCH // GB
GTILES = GT // TP
CN = 4
NC = NS // CN
KI = NC * MD
CW = CN * GT
PADL = L + 6

NE = 8
FF = 4 * D
FM = FF // 128
ST = 128
UN = 4
ETILES = -(-((2 * TOK - NE) // ST + NE) // UN) * UN
YG = 8
FAR = float(1 << 20)
EPS = 1e-5

POOL_STEPS = (0, 3, 6, 9)


def made_by(steps, it, k):
    return it * len(steps) + len([s for s in steps if s <= k])


VEC_STEPS = tuple(k for k in range(KI) if k not in POOL_STEPS)


def need(eng, sem, value):
    if not isinstance(value, int) or value > 0:
        eng.wait_ge(sem, value)


def fusion_kernel(nc, a, out):
    ctx = ExitStack()
    with ctx:
        def sb(name, shape, dt=F32):
            return ctx.enter_context(nc.sbuf_tensor(name, shape, dt))

        def sem(name):
            return ctx.enter_context(nc.semaphore(name))

        h = sb("h", [128, NT, D])
        xT = sb("xT", [128, 2, TOK])
        ident = sb("ident", [128, 128])
        stats = sb("stats", [128, NT, 6])
        mean = sb("mean", [128, NT])
        rstd = sb("rstd", [128, NT])
        lnt = sb("lnt", [128, 4, NT])
        zeros = sb("zeros", [128, D])
        in_w = sb("in_w", [128, 2, 2, 2 * DI])
        xp_w = sb("xp_w", [128, 2, MD, XP])
        dt_w = sb("dt_w", [128, 2, DI])
        out_w = sb("out_w", [128, 2, MD, D])
        conv_w = sb("conv_w", [128, 2, MD, 4])
        chan = sb("chan", [128, 2, 3, MD])
        negA = sb("negA", [128, 2, MD, NS])
        diagD = sb("diagD", [128, 2, MD, 128])
        upad = sb("upad", [128, MD, GB, PADL])
        acts = sb("acts", [128, 4, 2, MD, GT])
        us, sz, delta, du = (acts[:, i] for i in range(4))
        dbl = sb("dbl", [128, GT])
        bc = sb("bc", [128, 2, 2, CW])
        dA = sb("dA", [128, 2, CW])
        X = sb("X", [128, 3, CW])
        bcf = bc[:, :, :, :].rearrange("p a b n -> p (a b n)")
        Xf = X[:, :, :].rearrange("p a n -> p (a n)")
        dAf = dA[:, :, :].rearrange("p a n -> p (a n)")
        patches = bcf[:, 0:PK * 1024].rearrange("p (c n) -> p c n", c=PK)
        proj_w = bcf[:, PK * 1024:PK * 1024 + PK * D].rearrange("p (c n) -> p c n", c=PK)
        emb = Xf[:, 0:ET * D].rearrange("p (j d) -> p j d", j=ET)
        xn = Xf[:, ET * D:(ET + NT) * D].rearrange("p (j d) -> p j d", j=NT)
        embrow = dAf[:, 0:3 * D].rearrange("p (r d) -> p r d", r=3)
        spare = acts[:, :, :, :, :].rearrange("p i s m n -> p (i s m n)")
        taken = [0]

        def view(*dims):
            n, o = int(np.prod(dims)), taken[0]
            taken[0] += n
            names = "abc"[:len(dims)]
            return spare[:, o:o + n].rearrange(f"p ({' '.join(names)}) -> p {' '.join(names)}", **dict(zip(names, dims)))

        xa = Xf[:, 0:NT * D].rearrange("p (j d) -> p j d", j=NT)
        yg = Xf[:, NT * D:NT * D + YG * D].rearrange("p (s d) -> p s d", s=YG)
        w1 = bcf[:, 0:UN * 2 * FF].rearrange("p (s c f) -> p s c f", s=UN, c=2)
        w2 = view(UN, FM * D + FM)
        b2row = view(UN, D)
        mid = view(2, FM, ST)
        xg = view(UN, D)
        xgT = view(2, 2, ST)
        ye = view(UN, D)
        hr = view(2, 2, HG)
        wr1, wr2, br1, br2 = view(2, D), view(2, NE), view(2), view(NE)
        score, gate, chosen, pos, tmp, cum, cnt = (view(NT, NE) for _ in range(7))
        rowmax, rowsum, ones_j = view(NT), view(NT), view(NT)
        counts, padded, ends, starts = (view(NE) for _ in range(4))
        padded_i = view(NE).bitcast(I32)
        where = view(2, NT)
        where_i = view(2, NT).bitcast(U32)
        share = view(2, NT)
        texp = view(ETILES)
        texp_i = view(ETILES).bitcast(I32)
        tri = view(2, TP)
        tstart = view(ETILES)

        pg = ctx.enter_context(nc.psum_tensor("pg", [128, 2, 2, 512], F32))
        py = ctx.enter_context(nc.psum_tensor("py", [128, 4, 512], F32))

        scratch = nc.dram_tensor("bc_rows", (2 * NG, 2 * NS, GT), F32, kind="Internal").ap()
        xs = nc.dram_tensor("rows_by_expert", (ETILES * ST, D), F32, kind="Internal").ap()
        ys = nc.dram_tensor("outputs_by_expert", (ETILES * ST, D), F32, kind="Internal").ap()

        ld_emb, ld_txt, ld_w = sem("ld_emb"), sem("ld_txt"), sem("ld_w")
        ld_patch = [sem("ld_patch_first"), sem("ld_patch_rest")]
        emb_h = [sem("emb_h_first"), sem("emb_h_rest")]
        emb_mm, emb_st, emb_dn = sem("emb_mm"), sem("emb_st"), sem("emb_dn")
        ln_chain, ln_sqrt, ln_in, ln_xn, ln_tr = (
            sem("ln_chain"), sem("ln_sqrt"), sem("ln_in"), sem("ln_xn"), sem("ln_tr"))
        ln_cp_act, ln_cp_vec = sem("ln_cp_act"), sem("ln_cp_vec")
        passed = sem("passed")
        aexp, aneg, diag_rdy = sem("aexp"), sem("aneg"), sem("diag_rdy")
        u_mm, z_mm, xp_mm, dt_mm = sem("u_mm"), sem("z_mm"), sem("xp_mm"), sem("dt_mm")
        y_mm, op_mm = sem("y_mm"), sem("op_mm")
        u_cp, us_rdy, sz_rdy, dbl_rdy = sem("u_cp"), sem("us_rdy"), sem("sz_rdy"), sem("dbl_rdy")
        x_cp, exp_d, sp_rdy, dA_rdy = sem("x_cp"), sem("exp_d"), sem("sp_rdy"), sem("dA_rdy")
        tap_act, tap_d, conv_d = sem("tap_act"), sem("tap_d"), sem("conv_d")
        dbu_d, scan_d, hc_vec, y_part, h_add = (
            sem("dbu_d"), sem("scan_d"), sem("hc_vec"), sem("y_part"), sem("h_add"))
        zero_col = sem("zero_col")
        hc_pool, delta_d, du_d = sem("hc_pool"), sem("delta_d"), sem("du_d")
        bc_st = sem("bc_st")
        bc_ld = [sem("bc_ld0"), sem("bc_ld1")]
        ld_r, zero_d, filled = sem("ld_r"), sem("zero_d"), sem("filled")
        r_mm, r_act, s_mm, s_cp, top_in, r_exp, cnt_mm, cnt_cp, pos_rdy, tab_rdy, share_rdy = (
            sem("r_mm"), sem("r_act"), sem("s_mm"), sem("s_cp"), sem("top_in"), sem("r_exp"), sem("cnt_mm"),
            sem("cnt_cp"), sem("pos_rdy"), sem("tab_rdy"), sem("share_rdy"))
        xa_rdy, xa_tr, xa_cp, scattered = sem("xa_rdy"), sem("xa_tr"), sem("xa_cp"), sem("scattered")
        ld_x = [sem(f"ld_x{i}") for i in range(UN)]
        ld_we = [sem(f"ld_we{i}") for i in range(UN)]
        xg_tr, xg_cp, m_mm, m_act, e_mm, ye_cp = (
            sem("xg_tr"), sem("xg_cp"), sem("m_mm"), sem("m_act"), sem("e_mm"), sem("ye_cp"))
        ye_st = [sem(f"ye_st{i}") for i in range(UN)]
        gathered = [sem(f"gathered{i}") for i in range(YG)]
        moe_add, stored = sem("moe_add"), sem("stored")

        block = ctx.enter_context(nc.Block())

        def apart(eng):
            eng.sem_inc(passed, 1)

        def y_pieces(m):
            q, left, t, found = m * GB, GB, 0, []
            while left:
                n = min(left, 3 - q % 3)
                found.append((q // 3, (q % 3) * L, t * L, n * L))
                q, left, t = q + n, left - n, t + n
            return found

        @block.sync
        def _(sp):
            first = GB * IMG_TOK
            sp.dma_start(proj_w, a["proj_wT"].rearrange("(c p) n -> p c n", p=128)).then_inc(ld_patch[0], 16)
            for q, cols in enumerate((slice(0, first), slice(first, BATCH * IMG_TOK))):
                sp.dma_start(patches[:, :, cols], a["patches"].rearrange("(c p) n -> p c n", p=128)[:, :, cols]).then_inc(ld_patch[q], 16)
                if q == 0:
                    for r, name in enumerate(("proj_b", "gamma", "beta")):
                        sp.dma_start(embrow[:, r, :], a[name].partition_broadcast(128)).then_inc(ld_emb, 16)
            for d, p in enumerate("fb"):
                sp.dma_start(in_w[0:KD, d], a[p + "_in_wT"].rearrange("(c p) n -> p c n", p=KD)).then_inc(ld_w, 16)
                sp.dma_start(xp_w[:, d], a[p + "_xproj_wT"].rearrange("(c p) n -> p c n", p=128)).then_inc(ld_w, 16)
                sp.dma_start(dt_w[0:RANK, d], a[p + "_dt_wT"]).then_inc(ld_w, 16)
                sp.dma_start(out_w[:, d], a[p + "_out_wT"].rearrange("(c p) n -> p c n", p=128)).then_inc(ld_w, 16)
                sp.dma_start(conv_w[:, d], a[p + "_conv_w"].rearrange("(m p) k -> p m k", p=128)).then_inc(ld_w, 16)
                sp.dma_start(negA[:, d], a[p + "_Alog"].rearrange("(m p) n -> p m n", p=128)).then_inc(ld_w, 16)
                sp.dma_start(chan[:, d], a[p + "_chan"]).then_inc(ld_w, 16)
            for q, (e0, e1) in enumerate(((0, 2), (2, ET))):
                sp.wait_ge(emb_dn, q + 1)
                with nc.allow_non_contiguous_dma(reason="rows of 768 bytes"):
                    for o, p0, p1, q0 in ((0, 0, 64, 0), (1, 47, 79, 64), (1, 79, 94, 96), (2, 0, 16, 111), (2, 16, 17, 127)):
                        sp.dma_start(h[p0:p1, 3 * e0 + o:3 * e1:3, :], emb[q0:q0 + p1 - p0, e0:e1, :]).then_inc(emb_h[q], 16)

            def store_rows(g, d):
                it = 2 * g + d
                sp.wait_ge(dbl_rdy, it + 1)
                apart(sp)
                sp.dma_start(scratch[bass.ds(it, 1), :, :].rearrange("o n t -> (o n) t"),
                             dbl[RANK:XP, :]).then_inc(bc_st, 16)

            def load_chunk(g, d, c):
                it, s = 2 * g + d, c % 2
                need(sp, dbu_d, KI * it + MD * (c - 2) + MD)
                apart(sp)
                need(sp, hc_vec, made_by(VEC_STEPS, it, MD * (c - 2) + MD - 1) if c >= 2 else
                     made_by(VEC_STEPS, it - 1, MD * (c + 2) + MD - 1))
                apart(sp)
                need(sp, hc_pool, made_by(POOL_STEPS, it, MD * (c - 2) + MD - 1) if c >= 2 else
                     made_by(POOL_STEPS, it - 1, MD * (c + 2) + MD - 1))
                apart(sp)
                sp.wait_ge(bc_st, 16 * (it + 1))
                apart(sp)
                rows = scratch[bass.ds(it, 1), :, :].rearrange("o n t -> (o n) t")
                for w in range(2):
                    src = rows[w * NS + CN * c:w * NS + CN * (c + 1), :].rearrange("n t -> (n t)")
                    sp.dma_start(bc[:, s, w, :], src.partition_broadcast(128)).then_inc(bc_ld[s], 16)

            def group(g, last):
                for d in range(2):
                    for c in (2, 3):
                        load_chunk(g, d, c)
                    if d == 0 or not last:
                        n = (g, 1) if d == 0 else (g + 1, 0)
                        store_rows(*n)
                        load_chunk(*n, 0)
                        load_chunk(*n, 1)

            store_rows(0, 0)
            load_chunk(0, 0, 0)
            load_chunk(0, 0, 1)
            sp.wait_ge(zero_d, 1)
            sp.dma_start(xs.rearrange("(t p) d -> p t d", p=ST), zeros[:, :].unsqueeze(1).to_broadcast([128, ETILES, D])).then_inc(filled, 16)
            group(0, False)
            with sp.Fori(1, NG - 1) as g:
                group(g, False)
            group(NG - 1, True)

            sp.wait_ge(y_part, 2 * NG * 6)
            sp.wait_ge(op_mm, 2 * 2 * NG)
            for dst, name in ((wr1[0:KD], "Wr1T"), (wr2[0:KD], "Wr2T")):
                sp.dma_start(dst, a[name].rearrange("(c p) n -> p c n", p=KD)).then_inc(ld_r, 16)
            with nc.allow_non_contiguous_dma(reason="small vectors"):
                sp.dma_start(br1[0:KD], a["br1"].rearrange("(c p) -> p c", p=KD)).then_inc(ld_r, 16)
            sp.dma_start(br2, a["br2"].partition_broadcast(128)).then_inc(ld_r, 16)
            sp.dma_start(tri[0:TP], a["tri"]).then_inc(ld_r, 16)
            sp.dma_start(tstart[0:1], a["tstart"]).then_inc(ld_r, 16)

            sp.wait_ge(tab_rdy, 1)

            def load_tile(t, s):
                e = sp.value_load(texp_i[0:1, bass.ds(t, 1)], min_val=0, max_val=NE - 1)
                sp.dma_start(w1[0:KD, s], a["W1T"][bass.ds(e, 1)].rearrange("o (c p) f -> p (o c) f", p=KD)).then_inc(ld_we[s], 16)
                sp.dma_start(w2[:, s], a["W2b1"][bass.ds(e, 1)].rearrange("o p f -> p (o f)")).then_inc(ld_we[s], 16)
                sp.dma_start(b2row[:, s], a["b2"][bass.ds(e, 1)].rearrange("o d -> (o d)").partition_broadcast(128)).then_inc(ld_we[s], 16)

            def load_rows(t, s):
                sp.dma_start(xg[:, s], xs.rearrange("(t p) d -> t p d", p=ST)[bass.ds(t, 1)].rearrange("o p d -> p (o d)")).then_inc(ld_x[s], 16)

            for s in range(UN):
                load_tile(s, s)
            sp.wait_ge(scattered, 16 * 2 * NT)
            for s in range(UN):
                load_rows(s, s)
            with sp.Fori(1, ETILES // UN) as i:
                for s in range(UN):
                    t = i * UN + s
                    sp.wait_ge(ye_cp, t - UN + 1)
                    apart(sp)
                    load_tile(t, s)
                    load_rows(t, s)
            for q in range(4):
                j0, j1 = NT // 4 * q, NT // 4 * (q + 1)
                sp.wait_ge(moe_add, 2 * j1)
                sp.dma_start(out.rearrange("b t d -> (b t) d").rearrange("(j p) d -> p j d", p=TP)[:, j0:j1], h[0:TP, j0:j1]).then_inc(stored, 16)
            sp.wait_ge(stored, 64)

        @block.scalar
        def _(act):
            act.dma_start(ident[:, :], a["ident"]).then_inc(ld_txt, 16)
            txt = a["txt"]
            with nc.allow_non_contiguous_dma(reason="rows of 768 bytes"):
                act.dma_start(h[64:94, 0::3, :], txt[0::2, 0:30, :].rearrange("b t d -> t b d")).then_inc(ld_txt, 16)
                act.dma_start(h[0:47, 1::3, :], txt[0::2, 30:77, :].rearrange("b t d -> t b d")).then_inc(ld_txt, 16)
                act.dma_start(h[17:94, 2::3, :], txt[1::2, :, :].rearrange("b t d -> t b d")).then_inc(ld_txt, 16)
            def root(n, rows, j0, count):
                act.wait_ge(ln_in, n)
                nc.scalar.activation(rstd[0:rows, j0:j0 + count], rstd[0:rows, j0:j0 + count], ACT.Sqrt).then_inc(ln_sqrt, 1)

            def copy_u(it, tiles):
                for m in tiles:
                    act.wait_ge(u_mm, MD * it + m + 1)
                    need(act, conv_d, MD * (it - 1) + m + 1)
                    nc.scalar.activation(
                        upad[:, m, :, 3:3 + L].rearrange("p (a b) t -> p a b t", a=2),
                        pg[:, m % 2, :, 0:HG].rearrange("p a (b t) -> p a b t", b=2), ACT.Copy).then_inc(u_cp, 1)

            def first_tap(it, s, d, tiles):
                need(act, op_mm, 2 * (it - 1))
                for m in tiles:
                    act.wait_ge(u_cp, MD * it + m + 1)
                    o = 0 if d == 0 else 6
                    nc.scalar.activation(us[:, s, m, :].rearrange("p (b t) -> p b t", b=GB), upad[:, m, :, o:o + L], ACT.Identity,
                                         bias=chan[:, d, 0, m:m + 1], scale=conv_w[:, d, m, 0:1]).then_inc(tap_act, 1)

            def silu_u(it, s):
                for m in range(MD):
                    act.wait_ge(conv_d, MD * it + m + 1)
                    nc.scalar.activation(us[:, s, m, :], us[:, s, m, :], ACT.Silu).then_inc(us_rdy, 1)

            def silu_z(it, s, tiles):
                for m in tiles:
                    act.wait_ge(z_mm, MD * it + m + 1)
                    if m == 0:
                        need(act, y_part, 6 * (it - 1))
                    nc.scalar.activation(sz[:, s, m, :].rearrange("p (a n) -> p a n", a=2),
                                         pg[:, (m + 1) % 2, :, 0:HG], ACT.Silu).then_inc(sz_rdy, 1)

            def copy_dbl(it):
                act.wait_ge(xp_mm, it + 1)
                need(act, dt_mm, MD * it)
                need(act, bc_st, 16 * it)
                nc.scalar.activation(dbl[0:XP, :].rearrange("p (a n) -> p a n", a=2),
                                     pg[0:XP, 0, :, 0:HG], ACT.Copy).then_inc(dbl_rdy, 1)

            def abs_relu(it, s, d, tiles):
                for m in tiles:
                    act.wait_ge(dt_mm, MD * it + m + 1)
                    if m == 0:
                        need(act, du_d, MD * (it - 1))
                        need(act, dA_rdy, KI * (it - 1))
                        need(act, dbu_d, KI * (it - 1))
                    for dst, f in ((delta, ACT.Abs), (du, ACT.Relu)):
                        last = nc.scalar.activation(dst[:, s, m, :].rearrange("p (a n) -> p a n", a=2),
                                                    pg[:, (m + 1) % 2, :, 0:HG], f, bias=chan[:, d, 1, m:m + 1])
                    last.then_inc(x_cp, 1)

            def softplus(it, s):
                act.wait_ge(x_cp, MD * (it + 1))
                nc.scalar.activation(delta[:, s], delta[:, s], ACT.Exp, scale=-1.0).then_inc(exp_d, 1)
                act.wait_ge(exp_d, it + 1)
                nc.scalar.activation(delta[:, s], delta[:, s], ACT.Ln, bias=1.0).then_inc(sp_rdy, 1)

            def decay(it, s, d, k):
                c, m = k // MD, k % MD
                if k < MD:
                    act.wait_ge(delta_d, MD * it + m + 1)
                need(act, scan_d, KI * it + k - 1)
                rows = dA[:, k % 2, :].rearrange("p (n b t) -> p n b t", n=CN, b=GB)
                src = delta[:, s, m, :].rearrange("p (b t) -> p b t", b=GB)
                t0, t1 = (1, L) if d == 0 else (0, L - 1)
                for n in range(CN):
                    last = nc.scalar.activation(rows[:, n, :, t0:t1], src[:, :, t0:t1], ACT.Exp,
                                                scale=negA[:, d, m, CN * c + n:CN * c + n + 1])
                last.then_inc(dA_rdy, 1)

            def group(g, last):
                for d in range(2):
                    it = 2 * g + d
                    more = d == 0 or not last
                    for k in range(KI):
                        decay(it, d, d, k)
                        if more and k == 2:
                            copy_u(it + 1, (0, 1))
                        if more and k == 3:
                            copy_u(it + 1, (2,))
                        if more and k == 4:
                            first_tap(it + 1, 1 - d, 1 - d, range(MD))
                        if more and k == 6:
                            silu_u(it + 1, 1 - d)
                            silu_z(it + 1, 1 - d, (0, 1))
                        if more and k == 8:
                            copy_dbl(it + 1)
                            silu_z(it + 1, 1 - d, (2,))
                        if more and k == 10:
                            abs_relu(it + 1, 1 - d, 1 - d, (0, 1))
                        if more and k == 11:
                            abs_relu(it + 1, 1 - d, 1 - d, (2,))
                            softplus(it + 1, 1 - d)

            root(1, 128, NT - ET, 2)
            root(2, TP, 0, GTILES)
            for s in range(2):
                act.wait_ge(ln_tr, s + 1)
                nc.scalar.activation(xT[0:KD, :, s * HG:(s + 1) * HG], py[0:KD, 2 * s:2 * s + 2, 0:HG], ACT.Copy).then_inc(ln_cp_act, 1)
            root(3, 128, NT - ET + 2, ET - 2)
            act.wait_ge(ld_w, 16 * 14)
            nc.scalar.activation(negA[:, :, :, :], negA[:, :, :, :], ACT.Exp).then_inc(aexp, 1)
            for m in range(MD):
                copy_u(0, (m,))
                first_tap(0, 0, 0, (m,))
            silu_u(0, 0)
            silu_z(0, 0, range(MD))
            root(4, TP, GTILES, NT - GTILES)
            act.wait_ge(aneg, 1)
            copy_dbl(0)
            abs_relu(0, 0, 0, range(MD))
            softplus(0, 0)
            group(0, False)
            with act.Fori(1, NG - 1) as g:
                group(g, False)
            group(NG - 1, True)

            root(5, TP, 0, NT)
            for q in range(2 * NG):
                act.wait_ge(xa_tr, q + 1)
                nc.scalar.activation(xT[0:KD, :, HG * q:HG * (q + 1)], pg[0:KD, q % 2, :, 0:HG], ACT.Copy).then_inc(xa_cp, 1)
            act.wait_ge(ld_r, 16 * 6)
            with act.Fori(0, NG) as q2:
                for s in range(2):
                    act.wait_ge(r_mm, 2 * q2 + s + 1)
                    for c in range(2):
                        last = nc.scalar.activation(hr[0:KD, s, c, :], pg[0:KD, s, c, 0:HG], ACT.Relu, bias=br1[0:KD, c:c + 1])
                    last.then_inc(r_act, 1)
            act.wait_ge(top_in, 1)
            nc.scalar.activation(gate[0:TP], gate[0:TP], ACT.Exp).then_inc(r_exp, 1)

            def relu_tile(t, s):
                for bank, fs in ((0, range(0, 4)), (1, range(4, FM))):
                    act.wait_ge(m_mm, 2 * t + bank + 1)
                    for f in fs:
                        last = nc.scalar.activation(mid[:, s % 2, f, :], pg[:, s % 2, bank, ST * (f % 4):ST * (f % 4 + 1)], ACT.Relu,
                                                    bias=w2[:, s, FM * D + f:FM * D + f + 1])
                    last.then_inc(m_act, 1)

            with act.Fori(0, ETILES // UN) as i:
                for s in range(UN):
                    relu_tile(i * UN + s, s)

        @block.tensor
        def _(pe):
            for j in range(ET):
                if j == 0:
                    pe.wait_ge(ld_patch[0], 32)
                if j == 2:
                    pe.wait_ge(ld_patch[1], 16)
                need(pe, emb_st, j - 1)
                for c in range(PK):
                    last = nc.tensor.matmul(pg[:, j % 2, 0, 0:D], patches[:, c, 128 * j:128 * (j + 1)], proj_w[:, c, :],
                                            start=(c == 0), stop=(c == PK - 1))
                last.then_inc(emb_mm, 1)

            def transposes(n):
                pe.wait_ge(ln_xn, n + 1)
                for c in range(2):
                    for j in range(3):
                        last = nc.tensor.transpose(py[0:KD, 2 * (n % 2) + c, TP * j:TP * (j + 1)],
                                                   xn[0:TP, 3 * n + j, KD * c:KD * (c + 1)], ident[0:TP, 0:TP])
                last.then_inc(ln_tr, 1)

            pe.wait_ge(ld_txt, 64)
            for n in range(2):
                transposes(n)
            pe.wait_ge(ln_cp_act, 2)
            pe.wait_ge(emb_st, ET)
            pe.wait_ge(ld_w, 16 * 14)

            def in_proj(g, d, m, slot):
                apart(pe)
                for half in range(2):
                    for c in range(2):
                        last = nc.tensor.matmul(pg[:, slot, half, 0:HG], in_w[0:KD, d, c, 128 * m:128 * (m + 1)],
                                                xT[0:KD, c, bass.ds(g * GT + half * HG, HG)],
                                                start=(c == 0), stop=(c == 1))
                return last

            def proj_u(g, d, m):
                it = 2 * g + d
                if m == 0:
                    need(pe, x_cp, MD * (it - 1) + 2)
                if m == 1:
                    need(pe, x_cp, MD * it)
                if m == 2:
                    pe.wait_ge(u_cp, MD * it + 1)
                in_proj(g, d, m, m % 2).then_inc(u_mm, 1)

            def proj_z(g, d, m):
                it = 2 * g + d
                if m == 0:
                    pe.wait_ge(u_cp, MD * it + 2)
                    need(pe, h_add, 2 * (it - 1) - 1)
                if m == 1:
                    pe.wait_ge(u_cp, MD * it + 3)
                    need(pe, h_add, 2 * (it - 1))
                if m == 2:
                    pe.wait_ge(sz_rdy, MD * it + 1)
                in_proj(g, d, MD + m, (m + 1) % 2).then_inc(z_mm, 1)

            def xproj(g, d):
                it = 2 * g + d
                pe.wait_ge(us_rdy, MD * (it + 1))
                pe.wait_ge(sz_rdy, MD * it + 2)
                for half in range(2):
                    for m in range(MD):
                        last = nc.tensor.matmul(pg[0:XP, 0, half, 0:HG], xp_w[:, d, m, :],
                                                us[:, d, m, half * HG:(half + 1) * HG],
                                                start=(m == 0), stop=(m == MD - 1))
                last.then_inc(xp_mm, 1)

            def dt_proj(g, d, m):
                it = 2 * g + d
                if m == 0:
                    pe.wait_ge(dbl_rdy, it + 1)
                    pe.wait_ge(sz_rdy, MD * it + 3)
                if m == 2:
                    pe.wait_ge(x_cp, MD * it + 1)
                for half in range(2):
                    last = nc.tensor.matmul(pg[:, (m + 1) % 2, half, 0:HG], dt_w[0:RANK, d, 128 * m:128 * (m + 1)],
                                            dbl[0:RANK, half * HG:(half + 1) * HG], start=True, stop=True)
                last.then_inc(dt_mm, 1)

            def out_proj(it, d, part):
                tiles = (range(0, 4), range(4, GTILES))[part]
                if part == 0:
                    pe.wait_ge(y_part, 6 * (it + 1))
                for j in tiles:
                    o = j - tiles[0]
                    for m in range(MD):
                        last = nc.tensor.matmul(pg[0:TP, 1 - part, o // 2, D * (o % 2):D * (o % 2) + D],
                                                us[:, d, m, TP * j:TP * (j + 1)], out_w[:, d, m, :],
                                                start=(m == 0), stop=(m == MD - 1))
                last.then_inc(op_mm, 1)

            def sum_states(it, d, k):
                c, m = k // MD, k % MD
                first_in_bank = {0: (True, True), 1: (False, True), 2: (False, True)}[m]
                if c == 0:
                    need(pe, y_part, 6 * (it - 1) + (3, 5, 6)[m])
                    for (bank, col, tok, w), fresh in zip(y_pieces(m), first_in_bank):
                        nc.tensor.matmul(py[:, bank, col:col + w], diagD[:, d, m, :], us[:, d, m, tok:tok + w],
                                         start=fresh, stop=False, skip_group_check=True)
                if k in POOL_STEPS:
                    pe.wait_ge(hc_pool, made_by(POOL_STEPS, it, k))
                else:
                    pe.wait_ge(hc_vec, made_by(VEC_STEPS, it, k))
                for n in range(CN):
                    for bank, col, tok, w in y_pieces(m):
                        last = nc.tensor.matmul(py[:, bank, col:col + w], ident[:, :],
                                                X[:, k % 3, n * GT + tok:n * GT + tok + w],
                                                start=False, stop=(c == NC - 1 and n == CN - 1),
                                                skip_group_check=True)
                last.then_inc(y_mm, 1)

            def group(g, first, last):
                for d in range(2):
                    it = 2 * g + d
                    more = d == 0 or not last
                    prev = d == 1 or not first
                    n = (g, 1) if d == 0 else (g + 1, 0)
                    for k in range(KI):
                        if more:
                            if k == 0:
                                proj_u(*n, 0)
                                proj_u(*n, 1)
                            if k == 1:
                                proj_u(*n, 2)
                        if prev and k == 2:
                            if more:
                                pe.wait_ge(u_cp, MD * (it + 1) + 2)
                            else:
                                pe.wait_ge(x_cp, MD * (it + 1))
                            out_proj(it - 1, 1 - d, 0)
                            if more:
                                pe.wait_ge(u_cp, MD * (it + 1) + 3)
                            out_proj(it - 1, 1 - d, 1)
                        if more:
                            if k == 4:
                                proj_z(*n, 0)
                                proj_z(*n, 1)
                            if k == 6:
                                xproj(*n)
                                proj_z(*n, 2)
                            if k == 8:
                                dt_proj(*n, 0)
                                dt_proj(*n, 1)
                            if k == 9:
                                dt_proj(*n, 2)
                        sum_states(it, d, k)

            for m in range(MD):
                proj_u(0, 0, m)
            for m in range(MD):
                proj_z(0, 0, m)
            xproj(0, 0)
            for m in range(MD):
                dt_proj(0, 0, m)
            for n in range(2, 2 * NG):
                need(pe, ln_cp_vec, n - 3)
                transposes(n)
            pe.wait_ge(ln_cp_vec, 2 * NG - 2)
            pe.wait_ge(diag_rdy, 1)
            group(0, True, False)
            with pe.Fori(1, NG - 1) as g:
                group(g, False, False)
            group(NG - 1, False, True)
            pe.wait_ge(h_add, 2 * (2 * NG - 1))
            out_proj(2 * NG - 1, 1, 0)
            out_proj(2 * NG - 1, 1, 1)

            pe.wait_ge(h_add, 4 * NG)
            for j in range(NT):
                if j % 3 == 0:
                    need(pe, xa_cp, j // 3 - 1)
                pe.wait_ge(xa_rdy, j + 1)
                for c in range(2):
                    last = nc.tensor.transpose(pg[0:KD, j // 3 % 2, c, TP * (j % 3):TP * (j % 3 + 1)],
                                               xa[0:TP, j, KD * c:KD * (c + 1)], ident[0:TP, 0:TP])
                if j % 3 == 2:
                    last.then_inc(xa_tr, 1)
            pe.wait_ge(xa_cp, 2 * NG)
            pe.wait_ge(ld_r, 16 * 6)
            pe.wait_ge(y_part, 12 * NG)
            with pe.Fori(0, NG) as q2:
                for s in range(2):
                    for c in range(2):
                        for k in range(2):
                            last = nc.tensor.matmul(pg[0:KD, s, c, 0:HG], wr1[0:KD, k, KD * c:KD * (c + 1)],
                                                    xT[0:KD, k, bass.ds(q2 * GT + s * HG, HG)], start=(k == 0), stop=(k == 1))
                    last.then_inc(r_mm, 1)
                for s in range(2):
                    pe.wait_ge(r_act, 2 * q2 + s + 1)
                    for j in range(3):
                        for c in range(2):
                            last = nc.tensor.matmul(py[0:TP, s, NE * j:NE * (j + 1)], hr[0:KD, s, c, TP * j:TP * (j + 1)],
                                                    wr2[0:KD, c, :], start=(c == 0), stop=(c == 1))
                    last.then_inc(s_mm, 1)
                pe.wait_ge(s_cp, 2 * q2 + 2)
            pe.wait_ge(pos_rdy, 1)
            for b in range(2):
                last = nc.tensor.matmul(py[0:TP, b, 0:NT * NE], tri[0:TP, b, :], chosen[0:TP].rearrange("p j e -> p (j e)"),
                                        start=True, stop=True)
            last.then_inc(cnt_mm, 1)
            pe.wait_ge(cnt_cp, 1)

            def turn_rows(t, s):
                pe.wait_ge(ld_x[s], 16 * (t // UN + 1) if isinstance(t, int) else 16 * (t[0] + 1))
                for c in range(2):
                    last = nc.tensor.transpose(py[0:KD, s % 2, ST * c:ST * (c + 1)], xg[:, s, KD * c:KD * (c + 1)], ident[:, :])
                last.then_inc(xg_tr, 1)

            def second_layer(t, s, pieces):
                for f in range(FM):
                    if f == 0:
                        pe.wait_ge(m_act, 2 * t + 1)
                    if f == 4:
                        pe.wait_ge(m_act, 2 * t + 2)
                    last = nc.tensor.matmul(py[:, 2 + s % 2, 0:D], mid[:, s % 2, f, :], w2[:, s, D * f:D * (f + 1)],
                                            start=(f == 0), stop=(f == FM - 1))
                last.then_inc(e_mm, 1)

            def first_layer(t, s):
                pe.wait_ge(xg_cp, t + 1)
                for f in range(FM):
                    for c in range(2):
                        last = nc.tensor.matmul(pg[:, s % 2, f // 4, ST * (f % 4):ST * (f % 4 + 1)],
                                                w1[0:KD, s, c, 128 * f:128 * (f + 1)], xgT[0:KD, s % 2, c, :],
                                                start=(c == 0), stop=(c == 1))
                    if f in (3, FM - 1):
                        last.then_inc(m_mm, 1)

            def tiles(i, first):
                for s in range(UN):
                    t = i * UN + s
                    pe.wait_ge(ld_we[s], 48 * (i + 1))
                    turn_rows((i,), s)
                    if not (first and s == 0):
                        need(pe, ye_cp, t - 2)
                        second_layer(t - 1, (s - 1) % UN, None)
                    first_layer(t, s)

            tiles(0, True)
            with pe.Fori(1, ETILES // UN) as i:
                tiles(i, False)
            second_layer(ETILES - 1, UN - 1, None)

        @block.vector
        def _(dve):
            chain = [0]

            def then_next(ins):
                chain[0] += 1
                ins.then_inc(ln_chain, 1)
                dve.wait_ge(ln_chain, chain[0])

            nc.vector.memset(zeros[:, :], 0.0).then_inc(zero_d, 1)
            then_next(nc.vector.memset(upad[:, :, :, :], 0.0))

            def moments(n, rows, j0, count):
                js = slice(j0, j0 + count)
                st = stats[0:rows, js, :]
                s0, s1, s2 = (lnt[0:rows, i, 0:count] for i in range(3))
                then_next(nc.vector.tensor_tensor(s0, st[:, :, 1], st[:, :, 4], ALU.add))
                then_next(nc.vector.tensor_tensor(s1, st[:, :, 1], st[:, :, 4], ALU.subtract))
                then_next(nc.vector.tensor_tensor(s2, st[:, :, 2], st[:, :, 5], ALU.add))
                then_next(nc.vector.tensor_scalar(mean[0:rows, js], s0, 0.5, None, ALU.mult))
                then_next(nc.vector.scalar_tensor_tensor(s1, s1, 0.25, s1, ALU.mult, ALU.mult))
                then_next(nc.vector.scalar_tensor_tensor(s2, s2, 1.0 / D, s1, ALU.mult, ALU.add))
                nc.vector.tensor_scalar(rstd[0:rows, js], s2, EPS, None, ALU.add).then_inc(ln_in, 1)
                dve.wait_ge(ln_sqrt, n)
                then_next(nc.vector.reciprocal(rstd[0:rows, js], rstd[0:rows, js]))

            def embed(tiles):
                for j in tiles:
                    dve.wait_ge(emb_mm, j + 1)
                    nc.vector.tensor_tensor(emb[:, j, :], pg[:, j % 2, 0, 0:D], embrow[:, 0, :], ALU.add).then_inc(emb_st, 1)
                    dve.wait_ge(emb_st, j + 1)
                    last = nc.vector.bn_stats(stats[:, NT - ET + j, :], emb[:, j, :])
                then_next(last)

            def embed_norm(n, j0, j1):
                moments(n, 128, NT - ET + j0, j1 - j0)
                for j in range(j0, j1):
                    o = NT - ET + j
                    last = nc.vector.tensor_scalar(emb[:, j, :], emb[:, j, :], mean[:, o:o + 1], rstd[:, o:o + 1],
                                                   ALU.subtract, ALU.mult)
                then_next(last)
                row = lambda r: embrow[:, r, :].unsqueeze(1).to_broadcast([128, j1 - j0, D])
                then_next(nc.vector.tensor_tensor(emb[:, j0:j1, :], emb[:, j0:j1, :], row(1), ALU.mult))
                nc.vector.tensor_tensor(emb[:, j0:j1, :], emb[:, j0:j1, :], row(2), ALU.add).then_inc(emb_dn, 1)

            def statistics(n, j0, j1):
                for j in range(j0, j1):
                    last = nc.vector.bn_stats(stats[0:TP, j, :], h[0:TP, j, :])
                then_next(last)
                moments(n, TP, j0, j1 - j0)

            def normalise(j0, j1):
                for j in range(j0, j1):
                    last = nc.vector.tensor_scalar(xn[0:TP, j, :], h[0:TP, j, :], mean[0:TP, j:j + 1], rstd[0:TP, j:j + 1],
                                                   ALU.subtract, ALU.mult)
                    if j % 3 == 2:
                        last.then_inc(ln_xn, 1)

            dve.wait_ge(ld_emb, 48)
            embed(range(0, 2))
            embed_norm(1, 0, 2)
            embed(range(2, 5))
            dve.wait_ge(ld_txt, 64)
            dve.wait_ge(emb_h[0], 16 * 5)
            statistics(2, 0, GTILES)
            normalise(0, GTILES)
            embed(range(5, ET))
            embed_norm(3, 2, ET)
            dve.wait_ge(aexp, 1)
            nc.vector.tensor_scalar(negA[:, :, :, :], negA[:, :, :, :], -1.0, None, ALU.mult).then_inc(aneg, 1)
            for d in range(2):
                for m in range(MD):
                    last = nc.vector.tensor_scalar(diagD[:, d, m, :], ident[:, :], chan[:, d, 2, m:m + 1], None, ALU.mult)
            last.then_inc(diag_rdy, 1)

            def conv(it, s, d, tiles):
                for m in tiles:
                    dve.wait_ge(tap_act, MD * it + m + 1)
                    dst = us[:, s, m, :].rearrange("p (b t) -> p b t", b=GB)
                    for k in range(1, 4):
                        o = k if d == 0 else 6 - k
                        src = upad[:, m, :, o:o + L]
                        w = conv_w[:, d, m, k:k + 1]
                        if k > 1:
                            dve.wait_ge(tap_d, 2 * MD * it + 2 * m + k - 1)
                        nc.vector.scalar_tensor_tensor(dst, src, w, dst, ALU.mult, ALU.add)\
                            .then_inc(conv_d if k == 3 else tap_d, 1)

            def scan_step(it, s, d, k):
                c, m = k // MD, k % MD
                x = X[:, k % 3, :]
                xs = x.rearrange("p (n t) -> p n t", n=CN)
                if k < MD:
                    dve.wait_ge(du_d, MD * it + m + 1)
                if m == 0:
                    dve.wait_ge(bc_ld[c % 2], 64 * it + 32 * (c // 2) + 32)
                need(dve, y_mm, KI * it + k - 2)
                nc.vector.tensor_tensor(xs, du[:, s, m, :].unsqueeze(1).to_broadcast([128, CN, GT]),
                                        bc[:, c % 2, 0, :].rearrange("p (n t) -> p n t", n=CN), ALU.mult).then_inc(dbu_d, 1)
                if k < 2:
                    t0 = 0 if d == 0 else L - 1
                    need(dve, scan_d, KI * it + k - 1)
                    nc.vector.memset(dA[:, k % 2, :].rearrange("p (r t) -> p r t", t=L)[:, :, t0:t0 + 1], 0.0).then_inc(zero_col, 1)
                    dve.wait_ge(zero_col, 2 * it + k + 1)
                dve.wait_ge(dA_rdy, KI * it + k + 1)
                dve.wait_ge(dbu_d, KI * it + k + 1)
                dec = dA[:, k % 2, :]
                if d == 1:
                    x, dec = x[:, ::-1], dec[:, ::-1]
                nc.vector.tensor_tensor_scan(x, dec, x, 0.0, ALU.mult, ALU.add).then_inc(scan_d, 1)
                if k in VEC_STEPS:
                    dve.wait_ge(scan_d, KI * it + k + 1)
                    nc.vector.tensor_tensor(xs, xs, bc[:, c % 2, 1, :].rearrange("p (n t) -> p n t", n=CN), ALU.mult).then_inc(hc_vec, 1)

            def finish(it, s, d):
                dve.wait_ge(y_mm, KI * (it + 1))
                for m in range(MD):
                    for bank, col, tok, w in y_pieces(m):
                        nc.vector.tensor_tensor(us[:, s, m, tok:tok + w], py[:, bank, col:col + w],
                                                sz[:, s, m, tok:tok + w], ALU.mult).then_inc(y_part, 1)

            def add_out(g, it, part):
                tiles = (range(0, 4), range(4, GTILES))[part]
                n = len(tiles) // 2
                dve.wait_ge(op_mm, 2 * it + part + 1)
                need(dve, h_add, 2 * it + part)
                dst = h[0:TP, bass.ds(GTILES * g + tiles[0], 2 * n), :].rearrange("p (a b) d -> p a b d", a=n)
                nc.vector.tensor_tensor(dst, dst, pg[0:TP, 1 - part, 0:n, 0:2 * D].rearrange("p a (b d) -> p a b d", b=2),
                                        ALU.add).then_inc(h_add, 1)

            def group(g, first, last):
                for d in range(2):
                    it = 2 * g + d
                    more = d == 0 or not last
                    prev = d == 1 or not first
                    for k in range(KI):
                        if prev and k == 1:
                            finish(it - 1, 1 - d, 1 - d)
                        if prev and k == 4:
                            add_out(g - 1 if d == 0 else g, it - 1, 0)
                            add_out(g - 1 if d == 0 else g, it - 1, 1)
                        if more and k == 5:
                            conv(it + 1, 1 - d, 1 - d, range(MD))
                        scan_step(it, d, d, k)

            conv(0, 0, 0, range(MD))
            dve.wait_ge(emb_h[1], 16 * 5)
            statistics(4, GTILES, NT)
            normalise(GTILES, NT)
            for n in range(2, 2 * NG):
                dve.wait_ge(ln_tr, n + 1)
                nc.vector.tensor_copy(xT[0:KD, :, n * HG:(n + 1) * HG], py[0:KD, 2 * (n % 2):2 * (n % 2) + 2, 0:HG]).then_inc(ln_cp_vec, 1)
            dve.wait_ge(sp_rdy, 1)
            for m in range(MD):
                nc.vector.tensor_tensor(delta[:, 0, m], delta[:, 0, m], du[:, 0, m], ALU.add).then_inc(delta_d, 1)
                dve.wait_ge(delta_d, m + 1)
                nc.vector.tensor_tensor(du[:, 0, m], delta[:, 0, m], us[:, 0, m], ALU.mult).then_inc(du_d, 1)
            group(0, True, False)
            with dve.Fori(1, NG - 1) as g:
                group(g, False, False)
            group(NG - 1, False, True)
            finish(2 * NG - 1, 1, 1)
            add_out(NG - 1, 2 * NG - 1, 0)
            add_out(NG - 1, 2 * NG - 1, 1)
            dve.wait_ge(h_add, 4 * NG)

            statistics(5, 0, NT)
            for j in range(NT):
                nc.vector.tensor_scalar(xa[0:TP, j, :], h[0:TP, j, :], mean[0:TP, j:j + 1], rstd[0:TP, j:j + 1],
                                        ALU.subtract, ALU.mult).then_inc(xa_rdy, 1)
            dve.wait_ge(ld_r, 16 * 6)
            with dve.Fori(0, NG) as q2:
                for s in range(2):
                    dve.wait_ge(s_mm, 2 * q2 + s + 1)
                    nc.vector.tensor_tensor(score[0:TP, bass.ds(6 * q2 + 3 * s, 3), :],
                                            py[0:TP, s, 0:3 * NE].rearrange("p (j e) -> p j e", j=3),
                                            br2[0:TP, :].unsqueeze(1).to_broadcast([TP, 3, NE]), ALU.add).then_inc(s_cp, 1)
            dve.wait_ge(s_cp, 8)
            sc, rk, cm, gt, ps, cu, ct = (x[0:TP] for x in (score, chosen, tmp, gate, pos, cum, cnt))
            by_j = lambda x: x.unsqueeze(2).to_broadcast([TP, NT, NE])
            then_next(nc.vector.tensor_reduce(rowmax[0:TP], sc, AX.X, ALU.max))
            nc.vector.tensor_tensor(gt, sc, by_j(rowmax[0:TP]), ALU.subtract).then_inc(top_in, 1)
            then_next(nc.vector.memset(rk, 0.0))
            for o in range(NE):
                other = score[0:TP, :, o:o + 1]
                last = nc.vector.tensor_tensor(cm[:, :, 0:o + 1], other.to_broadcast([TP, NT, o + 1]), sc[:, :, 0:o + 1], ALU.is_gt)
                if o < NE - 1:
                    last = nc.vector.tensor_tensor(cm[:, :, o + 1:NE], other.to_broadcast([TP, NT, NE - 1 - o]), sc[:, :, o + 1:NE], ALU.is_ge)
                then_next(last)
                then_next(nc.vector.tensor_tensor(rk, rk, cm, ALU.add))
            nc.vector.tensor_scalar(rk, rk, 1.5, None, ALU.is_lt).then_inc(pos_rdy, 1)
            dve.wait_ge(pos_rdy, 1)
            then_next(nc.vector.memset(ones_j[0:TP], 1.0))
            dve.wait_ge(cnt_mm, 1)
            nc.vector.tensor_copy(ps, py[0:TP, 0, 0:NT * NE].rearrange("p (j e) -> p j e", e=NE))
            then_next(nc.vector.tensor_copy(ct, py[0:TP, 1, 0:NT * NE].rearrange("p (j e) -> p j e", e=NE)))
            for e in range(NE):
                last = nc.vector.tensor_tensor_scan(cu[:, :, e], ones_j[0:TP], ct[:, :, e], 0.0, ALU.mult, ALU.add)
            then_next(last)
            then_next(nc.vector.tensor_tensor(ct, cu, ct, ALU.subtract))
            then_next(nc.vector.tensor_tensor(ps, ps, ct, ALU.add))
            then_next(nc.vector.tensor_scalar(counts[0:TP], cu[:, NT - 1, :], float(ST - 1), None, ALU.add))
            then_next(nc.vector.tensor_copy(padded_i[0:TP], counts[0:TP]))
            then_next(nc.vector.tensor_scalar(padded_i[0:TP], padded_i[0:TP], -ST, None, ALU.bitwise_and))
            then_next(nc.vector.tensor_copy(padded[0:TP], padded_i[0:TP]))
            then_next(nc.vector.tensor_tensor_scan(ends[0:TP], ones_j[0:TP, 0:NE], padded[0:TP], 0.0, ALU.mult, ALU.add))
            then_next(nc.vector.tensor_tensor(starts[0:TP], ends[0:TP], padded[0:TP], ALU.subtract))
            then_next(nc.vector.tensor_tensor(ps, ps, starts[0:TP].unsqueeze(1).to_broadcast([TP, NT, NE]), ALU.add))
            then_next(nc.vector.tensor_scalar(cm, rk, -FAR, FAR, ALU.mult, ALU.add))
            then_next(nc.vector.tensor_tensor(cm, cm, ps, ALU.add))
            then_next(nc.vector.tensor_reduce(where[0:TP, 0, :], cm, AX.X, ALU.min))
            then_next(nc.vector.tensor_tensor(cm, ps, rk, ALU.mult))
            then_next(nc.vector.tensor_reduce(where[0:TP, 1, :], cm, AX.X, ALU.max))
            nc.vector.tensor_copy(where_i[0:TP], where[0:TP]).then_inc(cnt_cp, 1)
            then_next(nc.vector.memset(texp[0:1], 0.0))
            for e in range(NE - 1):
                then_next(nc.vector.scalar_tensor_tensor(texp[0:1], tstart[0:1], ends[0:1, e:e + 1], texp[0:1], ALU.is_ge, ALU.add))
            nc.vector.tensor_copy(texp_i[0:1], texp[0:1]).then_inc(tab_rdy, 1)
            dve.wait_ge(r_exp, 1)
            then_next(nc.vector.tensor_tensor(gt, gt, rk, ALU.mult))
            then_next(nc.vector.tensor_reduce(rowsum[0:TP], gt, AX.X, ALU.add))
            then_next(nc.vector.reciprocal(rowsum[0:TP], rowsum[0:TP]))
            then_next(nc.vector.tensor_tensor(gt, gt, by_j(rowsum[0:TP]), ALU.mult))
            for b in range(2):
                then_next(nc.vector.tensor_tensor(cm, ps, by_j(where[0:TP, b, :]), ALU.is_equal))
                then_next(nc.vector.tensor_tensor(cm, cm, gt, ALU.mult))
                then_next(nc.vector.tensor_reduce(share[0:TP, b, :], cm, AX.X, ALU.add))

            def copy_rows(t, s):
                dve.wait_ge(xg_tr, t + 1)
                nc.vector.tensor_copy(xgT[0:KD, s % 2], py[0:KD, s % 2, 0:2 * ST].rearrange("p (c n) -> p c n", c=2)).then_inc(xg_cp, 1)

            def copy_out(i, t, s, first):
                dve.wait_ge(e_mm, t + 1)
                if not first:
                    dve.wait_ge(ye_st[s], 16 * i)
                nc.vector.tensor_tensor(ye[:, s], py[:, 2 + s % 2, 0:D], b2row[:, s], ALU.add).then_inc(ye_cp, 1)

            def tiles(i, first):
                for s in range(UN):
                    copy_rows(i * UN + s, s)
                    if s > 0:
                        copy_out(i, i * UN + s - 1, s - 1, first)
                    elif not first:
                        copy_out(i - 1, i * UN - 1, UN - 1, isinstance(i, int) and i == 1)

            tiles(0, True)
            tiles(1, False)
            with dve.Fori(2, ETILES // UN) as i:
                tiles(i, False)
            copy_out(ETILES // UN - 1, ETILES - 1, UN - 1, False)
            for n in range(2 * NT):
                j, b = n // 2, n % 2
                dve.wait_ge(gathered[n % YG], 16 * (n // YG + 1))
                need(dve, moe_add, n if b else 0)
                nc.vector.scalar_tensor_tensor(h[0:TP, j, :], yg[0:TP, n % YG, :], share[0:TP, b, j:j + 1], h[0:TP, j, :],
                                               ALU.mult, ALU.add).then_inc(moe_add, 1)

        @block.gpsimd
        def _(pool):
            def softplus_sum(it, s):
                pool.wait_ge(sp_rdy, it + 1)
                pool.wait_ge(us_rdy, MD * (it + 1))
                for m in range(MD):
                    nc.gpsimd.tensor_tensor(delta[:, s, m], delta[:, s, m], du[:, s, m], ALU.add).then_inc(delta_d, 1)
                    pool.wait_ge(delta_d, MD * it + m + 1)
                    nc.gpsimd.tensor_tensor(du[:, s, m], delta[:, s, m], us[:, s, m], ALU.mult).then_inc(du_d, 1)

            def group(g, last):
                for d in range(2):
                    it = 2 * g + d
                    for k in POOL_STEPS:
                        c = k // MD
                        pool.wait_ge(scan_d, KI * it + k + 1)
                        x = X[:, k % 3, :]
                        pool.wait_ge(bc_ld[c % 2], 64 * it + 32 * (c // 2) + 32)
                        nc.gpsimd.tensor_tensor(x, x, bc[:, c % 2, 1, :], ALU.mult).then_inc(hc_pool, 1)
                    if d == 0 or not last:
                        softplus_sum(it + 1, 1 - d)

            group(0, False)
            with pool.Fori(1, NG - 1) as g:
                group(g, False)
            group(NG - 1, True)

            pool.wait_ge(filled, 16)
            pool.wait_ge(cnt_cp, 1)
            pool.wait_ge(xa_rdy, NT)
            for j in range(NT):
                for b in range(2):
                    pool.indirect_dma_start(xs, bass.IndirectOffsetOnAxis(where_i[0:TP, b, j:j + 1], 0), xa[0:TP, j, :], None).then_inc(scattered, 16)

            def store(i, s):
                pool.wait_ge(ye_cp, i * UN + s + 1)
                apart(pool)
                dst = ys.rearrange("(t p) d -> t p d", p=ST)[bass.ds(i * UN + s, 1)].rearrange("o p d -> p (o d)")
                pool.dma_start(dst, ye[:, s]).then_inc(ye_st[s], 16)

            with pool.Fori(0, ETILES // UN) as i:
                for s in range(UN):
                    store(i, s)
            for s in range(UN):
                pool.wait_ge(ye_st[s], 16 * (ETILES // UN))
            for n in range(2 * NT):
                j, b = n // 2, n % 2
                need(pool, moe_add, n - YG + 1)
                pool.indirect_dma_start(yg[0:TP, n % YG, :], None, ys, bass.IndirectOffsetOnAxis(where_i[0:TP, b, j:j + 1], 0)).then_inc(gathered[n % YG], 16)


def kernel(**inputs):
    import concourse.bacc as bacc
    from concourse.bass_utils import run_bass_kernel_spmd

    v = {n: np.asarray(x) for n, x in inputs.items()}
    P = PATCH
    x = v["x"]
    hp, wp = x.shape[2] // P, x.shape[3] // P
    host = {
        "patches": x.reshape(BATCH, 3, hp, P, wp, P).transpose(1, 3, 5, 0, 2, 4).reshape(3 * P * P, BATCH * hp * wp),
        "txt": v["txt"], "proj_wT": v["L0_tok_W_proj"].T, "proj_b": v["L0_tok_b_proj"],
        "gamma": v["L0_tok_gamma"], "beta": v["L0_tok_beta"],
        "W1T": v["L0_ffn_W1"].transpose(0, 2, 1), 
        "W2b1": np.concatenate([v["L0_ffn_W2"].transpose(0, 2, 1).reshape(NE, FM, 128, D).transpose(0, 2, 1, 3).reshape(NE, 128, FM * D),
                                v["L0_ffn_b1"].reshape(NE, FM, 128).transpose(0, 2, 1)], axis=2),
        "tri": np.stack([np.triu(np.ones((TP, TP), np.float32), 1), np.ones((TP, TP), np.float32)], axis=1),
        "tstart": np.arange(0, ETILES * ST, ST, dtype=np.float32)[None],
        "b2": v["L0_ffn_b2"], "Wr1T": v["L0_ffn_Wr1"].T, "br1": v["L0_ffn_br1"],
        "Wr2T": v["L0_ffn_Wr2"].T, "br2": v["L0_ffn_br2"], "ident": np.eye(128, dtype=np.float32),
    }
    for p in "fb":
        w = {n: v[f"L0_attn_{p}_{n}"] for n in ("in_w", "conv_w", "conv_b", "xproj_w", "dt_w", "dt_b", "Alog", "D", "out_w")}
        host.update({p + "_in_wT": w["in_w"].T, p + "_xproj_wT": w["xproj_w"].T, p + "_dt_wT": w["dt_w"].T,
                     p + "_out_wT": w["out_w"].T, p + "_conv_w": w["conv_w"], p + "_Alog": w["Alog"],
                     p + "_chan": np.stack([w[n].reshape(MD, 128).T for n in ("conv_b", "dt_b", "D")], axis=1)})
    nc = bacc.Bacc("TRN2", target_bir_lowering=False, num_devices=1)
    arrays, aps = {}, {}
    for n, arr in host.items():
        arrays["in_" + n] = np.ascontiguousarray(arr)
        aps[n] = nc.dram_tensor("in_" + n, arrays["in_" + n].shape, F32, kind="ExternalInput").ap()
    out = nc.dram_tensor("out_0", (BATCH, L, D), F32, kind="ExternalOutput").ap()
    fusion_kernel(nc, aps, out)
    r = run_bass_kernel_spmd(nc, [arrays], core_ids=[0])
    return r.results[0]["out_0"]
```

```python
from contextlib import ExitStack

import numpy as np

import concourse.bass as bass
from concourse import mybir

F32 = mybir.dt.float32
BF16 = mybir.dt.bfloat16
I32 = mybir.dt.int32
U32 = mybir.dt.uint32
ALU = mybir.AluOpType
ACT = mybir.ActivationFunctionType
AX = mybir.AxisListType

BATCH, IMG_TOK, TXT_TOK = 16, 64, 77
L = IMG_TOK + TXT_TOK
TOK = BATCH * L
D = 192
KD = D // 2
TP = 94
NT = TOK // TP
PATCH = 16
PK = 3 * PATCH * PATCH // 128
ET = BATCH * IMG_TOK // 128

DI = 2 * D
MD = DI // 128
NS = 16
RANK = D // 16
XP = RANK + 2 * NS
GB = 4
GT = GB * L
HG = GT // 2
NG = BATCH // GB
GTILES = GT // TP
CP = 2
CN = 4
NC = NS // CN
KI = NC * MD
CW = CN * GT
PADL = L + 6

NE = 8
FF = 4 * D
FM = FF // 128
ST = 128
UN = 4
ETILES = (2 * TOK + NE * (ST - 1)) // ST
BODIES, REST = ETILES // UN, ETILES % UN
EW1, EW2 = 2 * FF, FM * D + FM
ER = 1 + 2 * TOK
Z_SLOT = (1, 0, 0)
QT = NT // 4
IDB = 64
FAR = float(1 << 20)
EPS = 1e-5

POOL_STEPS = (0, 1, 3, 4, 6, 7, 9, 10)
PN = 2


def by_pool(it, k):
    return it * len(POOL_STEPS) + len([s for s in POOL_STEPS if s <= k])


def uses(s):
    return len(range(s, ETILES, UN))


def need(eng, sem, value):
    if not isinstance(value, int) or value > 0:
        eng.wait_ge(sem, value)


def begins(it):
    return isinstance(it, int) and it == 0


def fusion_kernel(nc, a, out):
    ctx = ExitStack()
    with ctx:
        def sb(name, shape, dt=F32):
            return ctx.enter_context(nc.sbuf_tensor(name, shape, dt))

        def sem(name):
            return ctx.enter_context(nc.semaphore(name))

        h = sb("h", [128, NT, D])
        xT = sb("xT", [128, 2, TOK])
        ident = sb("ident", [128, 128])
        stats = sb("stats", [128, NT, 6])
        mean = sb("mean", [128, NT])
        rstd = sb("rstd", [128, NT])
        lnt = sb("lnt", [128, 4, NT])
        zeros = sb("zeros", [128, D])
        W_IN, W_BC, W_DA, W_X = 8 * DI, 4 * CW, 2 * CW, 3 * CW
        work = sb("work", [128, W_IN + W_BC + W_DA + W_X])
        in_w = work[:, 0:W_IN].rearrange("p (d c n) -> p d c n", d=2, c=2)
        xp_w = sb("xp_w", [128, 2, MD, XP])
        dt_w = sb("dt_w", [128, 2, DI])
        out_w = sb("out_w", [128, 2, MD, D])
        conv_w = sb("conv_w", [128, 2, MD, 4])
        chan = sb("chan", [128, 2, 3, MD])
        negA = sb("negA", [128, 2, MD, NS])
        diagD = sb("diagD", [128, 2, MD, 128])
        diag_conv = sb("diag_conv", [128, CP, 4, 128])
        upad = sb("upad", [128, MD, GB, PADL])
        acts = sb("acts", [128, 4, 2, MD, GT])
        us, sz, delta, du = (acts[:, i] for i in range(4))
        dbl = sb("dbl", [128, GT])
        bcf = work[:, W_IN:W_IN + W_BC]
        dAf = work[:, W_IN + W_BC:W_IN + W_BC + W_DA]
        Xf = work[:, W_IN + W_BC + W_DA:]
        bc = bcf.rearrange("p (s w n) -> p s w n", s=2, w=2)
        dA = dAf.rearrange("p (s n) -> p s n", s=2)
        X = Xf.rearrange("p (s n) -> p s n", s=3)
        patches = bcf[:, 0:PK * 1024].rearrange("p (c n) -> p c n", c=PK)
        proj_w = bcf[:, PK * 1024:PK * 1024 + PK * D].rearrange("p (c n) -> p c n", c=PK)
        emb = Xf[:, 0:ET * D].rearrange("p (j d) -> p j d", j=ET)
        xn = Xf[:, ET * D:(ET + NT) * D].rearrange("p (j d) -> p j d", j=NT)
        embrow = dAf[:, 0:3 * D].rearrange("p (r d) -> p r d", r=3)
        def cutter(flat, size):
            taken = [0]

            def piece(*dims):
                n, o = int(np.prod(dims)), taken[0]
                taken[0] += n
                assert taken[0] <= size
                names = "abc"[:len(dims)]
                return flat[:, o:o + n].rearrange(f"p ({' '.join(names)}) -> p {' '.join(names)}", **dict(zip(names, dims)))
            return piece

        US, SZ, DELTA, DU = range(4)
        item_buf = lambda i, s: cutter(acts[:, i, s].rearrange("p m n -> p (m n)"), MD * GT)
        xa_part = [item_buf(i, 0)(8, D) for i in (SZ, DELTA, DU)]
        xa = [xa_part[j // 8][:, j % 8, :] for j in range(NT)]
        piece = item_buf(US, 0)
        hr, wr1, wr2, br1, br2 = piece(2, 2, HG), piece(2, D), piece(2, NE), piece(2), piece(NE)
        piece = cutter(upad.rearrange("p m b t -> p (m b t)"), MD * GB * PADL)
        score, gate, chosen, pos, tmp, cum, cnt = (piece(NT, NE) for _ in range(7))
        rowmax, rowsum, ones_j = piece(NT), piece(NT), piece(NT)
        counts, padded, ends, starts = (piece(NE) for _ in range(4))
        padded_i = piece(NE).bitcast(I32)
        where = piece(2, NT)
        base, lo = (piece(NT).bitcast(BF16).rearrange("p (b j) -> p b j", b=2) for _ in range(2))
        lo_i = piece(2, NT).bitcast(I32)
        texp = piece(ETILES + 1)
        piece = cutter(dbl[:, :], GT)
        tri, iota, tstart, dump, ids = piece(2, TP), piece(ST), piece(ETILES + 1), piece(ETILES), piece(2, 2 * NT)
        texp_i = piece(ETILES + 1).bitcast(I32)
        piece = cutter(xp_w.rearrange("p d m x -> p (d m x)"), 2 * MD * XP)
        share = piece(2, NT)
        row_to, row_from = piece(ETILES), piece(ETILES)
        row_to_i, row_from_i = piece(ETILES).bitcast(U32), piece(ETILES).bitcast(U32)
        from_now, to_now = piece(UN).bitcast(U32), piece(UN).bitcast(U32)
        piece = item_buf(DU, 1)
        above = piece(NT, NE, NE)
        iota_h, tstart_h, ids_h = (piece(-(-n // 2)).bitcast(BF16)[:, 0:n] for n in (ST, ETILES, 2 * 2 * NT))
        ids_h = ids_h.rearrange("p (w n) -> p w n", w=2)
        piece = cutter(xT.rearrange("p c n -> p (c n)"), 2 * TOK)
        is_row = piece(2 * NT * ST // 2).bitcast(BF16).rearrange("p (n r) -> p n r", r=ST)
        is_tile = item_buf(US, 1)(2 * NT * ETILES // 2).bitcast(BF16).rearrange("p (n t) -> p n t", t=ETILES)
        id_tile = acts[:, SZ:DELTA + 1, 1].rearrange("p i m n -> p i (m n)")[:, :, 0:NT * ETILES].bitcast(BF16)\
            .rearrange("p w (n t) -> p w n t", t=ETILES)
        home = work[:, 0:NE * (EW1 + EW2 + D)].rearrange("p (e f) -> p e f", e=NE)
        w1 = [item_buf(i, 0)(2, FF) for i in (SZ, DU)]
        w2 = [item_buf(i, 0)(EW2 + D) for i in (DELTA, US)]
        mid = item_buf(SZ, 1)(2, FM, ST)
        piece = item_buf(DU, 1)
        xg, ye = piece(UN, D), piece(UN, D)
        xgT = item_buf(DELTA, 1)(2, 2, ST)
        piece = cutter(work[:, :], 4 * 2 * QT * D)
        yq = [piece(2, QT, D) for _ in range(4)]

        pg = ctx.enter_context(nc.psum_tensor("pg", [128, 2, 2, 512], F32))
        py = ctx.enter_context(nc.psum_tensor("py", [128, 4, 512], F32))

        scratch = nc.dram_tensor("bc_rows", (2 * NG, 2 * NS, GT), F32, kind="Internal").ap()
        xr = nc.dram_tensor("normalised", (1 + TOK, D), F32, kind="Internal").ap()
        ys = nc.dram_tensor("expert_outputs", (ER + ETILES * ST, D), F32, kind="Internal").ap()

        ld_emb, ld_txt, ld_w = sem("ld_emb"), sem("ld_txt"), sem("ld_w")
        ld_patch = [sem("ld_patch_first"), sem("ld_patch_rest")]
        emb_h = [sem("emb_h_first"), sem("emb_h_rest")]
        emb_mm, emb_st, emb_dn = sem("emb_mm"), sem("emb_st"), sem("emb_dn")
        ln_chain, ln_sqrt, ln_in, ln_xn, ln_tr = (
            sem("ln_chain"), sem("ln_sqrt"), sem("ln_in"), sem("ln_xn"), sem("ln_tr"))
        ln_cp_act, ln_cp_vec = sem("ln_cp_act"), sem("ln_cp_vec")
        passed = sem("passed")
        aexp, aneg, diag_rdy, taps_rdy, conv_mm = sem("aexp"), sem("aneg"), sem("diag_rdy"), sem("taps_rdy"), sem("conv_mm")
        u_mm, z_mm, xp_mm, dt_mm = sem("u_mm"), sem("z_mm"), sem("xp_mm"), sem("dt_mm")
        y_mm, op_mm = sem("y_mm"), sem("op_mm")
        u_cp, us_rdy, sz_rdy, dbl_rdy = sem("u_cp"), sem("us_rdy"), sem("sz_rdy"), sem("dbl_rdy")
        x_cp, exp_d, sp_rdy, dA_rdy = sem("x_cp"), sem("exp_d"), sem("sp_rdy"), sem("dA_rdy")
        tap_act, tap_d, conv_d = sem("tap_act"), sem("tap_d"), sem("conv_d")
        dbu_d, scan_d, hc_vec, y_part, h_add = (
            sem("dbu_d"), sem("scan_d"), sem("hc_vec"), sem("y_part"), sem("h_add"))
        zero_col = sem("zero_col")
        hc_pool, delta_d, du_d = sem("hc_pool"), sem("delta_d"), sem("du_d")
        bc_st = sem("bc_st")
        bc_ld = [sem("bc_ld0"), sem("bc_ld1")]
        ld_r, ld_c, zero_d = sem("ld_r"), sem("ld_c"), sem("zero_d")
        r_mm, r_act, s_mm, s_cp, top_in, r_exp, pos_rdy, cnt_mm, hot, id_mm, idx_rdy, tab_rdy, share_rdy = (
            sem("r_mm"), sem("r_act"), sem("s_mm"), sem("s_cp"), sem("top_in"), sem("r_exp"), sem("pos_rdy"),
            sem("cnt_mm"), sem("hot"), sem("id_mm"), sem("idx_rdy"), sem("tab_rdy"), sem("share_rdy"))
        xa_rdy, xa_tr, xa_cp, xa_st = sem("xa_rdy"), sem("xa_tr"), sem("xa_cp"), sem("xa_st")
        ld_home, w_rdy = sem("ld_home"), sem("w_rdy")
        ld_x = [sem(f"ld_x{i}") for i in range(UN)]
        xg_tr, xg_cp, m_mm, m_act, e_mm, ye_cp = (
            sem("xg_tr"), sem("xg_cp"), sem("m_mm"), sem("m_act"), sem("e_mm"), sem("ye_cp"))
        ye_st = [sem(f"ye_st{i}") for i in range(UN)]
        ld_y = [[sem(f"ld_y{i}{b}") for b in range(2)] for i in range(4)]
        first_add, scaled, hot_pool = sem("first_add"), sem("scaled"), sem("hot_pool")
        from_cp, to_cp = sem("from_cp"), sem("to_cp")
        moe_add, stored = sem("moe_add"), sem("stored")

        block = ctx.enter_context(nc.Block())

        PARTS = ((0, 80), (80, TP))

        def apart(eng):
            eng.sem_inc(passed, 1)

        def number_tiles(eng, n):
            half = NT // 2
            ns = slice(half * n, half * (n + 1))
            return eng.tensor_tensor(id_tile[0:TP, :, ns, :], is_tile[0:TP, ns, :].unsqueeze(1).to_broadcast([TP, 2, half, ETILES]),
                                     ids_h[0:TP, :, ns].unsqueeze(3).to_broadcast([TP, 2, half, ETILES]), ALU.mult)

        def y_pieces(m):
            q, left, t, found = m * GB, GB, 0, []
            while left:
                n = min(left, 3 - q % 3)
                found.append((q // 3, (q % 3) * L, t * L, n * L))
                q, left, t = q + n, left - n, t + n
            return found

        @block.sync
        def _(sp):
            first = GB * IMG_TOK
            sp.dma_start(proj_w, a["proj_wT"].rearrange("(c p) n -> p c n", p=128)).then_inc(ld_patch[0], 16)
            for q, cols in enumerate((slice(0, first), slice(first, BATCH * IMG_TOK))):
                sp.dma_start(patches[:, :, cols], a["patches"].rearrange("(c p) n -> p c n", p=128)[:, :, cols]).then_inc(ld_patch[q], 16)
                if q == 0:
                    for r, name in enumerate(("proj_b", "gamma", "beta")):
                        sp.dma_start(embrow[:, r, :], a[name].partition_broadcast(128)).then_inc(ld_emb, 16)
            for d, p in enumerate("fb"):
                sp.dma_start(in_w[0:KD, d], a[p + "_in_wT"].rearrange("(c p) n -> p c n", p=KD)).then_inc(ld_w, 16)
                sp.dma_start(xp_w[:, d], a[p + "_xproj_wT"].rearrange("(c p) n -> p c n", p=128)).then_inc(ld_w, 16)
                sp.dma_start(dt_w[0:RANK, d], a[p + "_dt_wT"]).then_inc(ld_w, 16)
                sp.dma_start(out_w[:, d], a[p + "_out_wT"].rearrange("(c p) n -> p c n", p=128)).then_inc(ld_w, 16)
                sp.dma_start(conv_w[:, d], a[p + "_conv_w"].rearrange("(m p) k -> p m k", p=128)).then_inc(ld_w, 16)
                sp.dma_start(negA[:, d], a[p + "_Alog"].rearrange("(m p) n -> p m n", p=128)).then_inc(ld_w, 16)
                sp.dma_start(chan[:, d], a[p + "_chan"]).then_inc(ld_w, 16)
            for q, (e0, e1) in enumerate(((0, 2), (2, ET))):
                sp.wait_ge(emb_dn, q + 1)
                with nc.allow_non_contiguous_dma(reason="rows of 768 bytes"):
                    for o, p0, p1, q0 in ((0, 0, 64, 0), (1, 47, 79, 64), (1, 79, 94, 96), (2, 0, 16, 111), (2, 16, 17, 127)):
                        sp.dma_start(h[p0:p1, 3 * e0 + o:3 * e1:3, :], emb[q0:q0 + p1 - p0, e0:e1, :]).then_inc(emb_h[q], 16)

            def store_rows(g, d):
                it = 2 * g + d
                sp.wait_ge(dbl_rdy, it + 1)
                apart(sp)
                sp.dma_start(scratch[bass.ds(it, 1), :, :].rearrange("o n t -> (o n) t"),
                             dbl[RANK:XP, :]).then_inc(bc_st, 16)

            def load_chunk(g, d, c):
                it, s = 2 * g + d, c % 2
                need(sp, dbu_d, KI * it + MD * (c - 2) + MD)
                apart(sp)
                need(sp, hc_vec, KI * it + MD * (c - 2) + MD)
                apart(sp)
                need(sp, hc_pool, by_pool(it, MD * (c - 2) + MD - 1) if c >= 2 else
                     by_pool(it - 1, MD * (c + 2) + MD - 1))
                apart(sp)
                sp.wait_ge(bc_st, 16 * (it + 1))
                apart(sp)
                rows = scratch[bass.ds(it, 1), :, :].rearrange("o n t -> (o n) t")
                for w in range(2):
                    src = rows[w * NS + CN * c:w * NS + CN * (c + 1), :].rearrange("n t -> (n t)")
                    sp.dma_start(bc[:, s, w, :], src.partition_broadcast(128)).then_inc(bc_ld[s], 16)

            def group(g, last):
                for d in range(2):
                    load_chunk(g, d, 2)
                    if last and d == 1:
                        load_router()
                    load_chunk(g, d, 3)
                    if d == 0 or not last:
                        n = (g, 1) if d == 0 else (g + 1, 0)
                        store_rows(*n)
                        load_chunk(*n, 0)
                        load_chunk(*n, 1)

            def load_router():
                sp.wait_ge(op_mm, 2 * (2 * NG - 1))
                for dst, name in ((wr1[0:KD], "Wr1T"), (wr2[0:KD], "Wr2T")):
                    sp.dma_start(dst, a[name].rearrange("(c p) n -> p c n", p=KD)).then_inc(ld_r, 16)
                with nc.allow_non_contiguous_dma(reason="small vectors"):
                    sp.dma_start(br1[0:KD], a["br1"].rearrange("(c p) -> p c", p=KD)).then_inc(ld_r, 16)
                sp.dma_start(br2, a["br2"].partition_broadcast(128)).then_inc(ld_r, 16)

            def store_xa(j0, j1):
                for p0, p1 in PARTS:
                    sp.dma_start(xr[1:1 + TOK, :].rearrange("(j p) d -> p j d", p=TP)[p0:p1, j0:j1],
                                 xa_part[j0 // 8][p0:p1, j0 % 8:j0 % 8 + j1 - j0]).then_inc(xa_st, 16)

            def load_home(e):
                sp.dma_start(home[0:KD, e, 0:EW1].rearrange("p (c f) -> p c f", c=2), a["W1T"][e].rearrange("(c p) f -> p c f", p=KD)).then_inc(ld_home, 16)
                sp.dma_start(home[:, e, EW1:EW1 + EW2], a["W2b1"][e]).then_inc(ld_home, 16)
                sp.dma_start(home[:, e, EW1 + EW2:], a["b2"][e].partition_broadcast(128)).then_inc(ld_home, 16)

            store_rows(0, 0)
            load_chunk(0, 0, 0)
            load_chunk(0, 0, 1)
            sp.wait_ge(zero_d, 1)
            sp.dma_start(xr[0:1, :], zeros[0:1, :]).then_inc(xa_st, 16)
            group(0, False)
            with sp.Fori(1, NG - 1) as g:
                group(g, False)
            group(NG - 1, True)

            sp.wait_ge(xa_rdy, 3 * GTILES)
            store_xa(0, 8)
            store_xa(8, 16)
            store_xa(16, 18)
            sp.wait_ge(dt_mm, 2 * NG * MD)
            sp.wait_ge(bc_st, 16 * 2 * NG)
            sp.dma_start(tri[0:TP], a["tri"]).then_inc(ld_c, 16)
            sp.dma_start(ids[0:TP], a["ids"]).then_inc(ld_c, 16)
            sp.dma_start(dump, a["dump"]).then_inc(ld_c, 16)
            for dst, name in ((iota, "iota"), (tstart, "tstart")):
                sp.dma_start(dst, a[name].partition_broadcast(128)).then_inc(ld_c, 16)
            sp.wait_ge(z_mm, 2 * NG * MD)
            sp.wait_ge(hc_vec, KI * (2 * NG - 1) + 3 * MD)
            sp.wait_ge(hc_pool, by_pool(2 * NG - 1, 3 * MD - 1))
            load_home(0)
            load_home(1)
            sp.wait_ge(y_mm, 2 * NG * KI)
            for e in range(2, NE):
                load_home(e)
            sp.wait_ge(xa_rdy, NT)
            store_xa(18, NT)

            for s in range(UN):
                sp.wait_ge(ye_st[s], 16 * uses(s))
            for q in range(4):
                for p0, p1 in PARTS:
                    sp.dma_start(yq[q][p0:p1, 0], ys[1:1 + TOK, :].rearrange("(j p) d -> p j d", p=TP)
                                 [p0:p1, QT * q:QT * (q + 1)]).then_inc(ld_y[q][0], 16)
            for q in range(4):
                sp.wait_ge(moe_add, q + 1)
                js = slice(QT * q, QT * (q + 1))
                for p0, p1 in PARTS:
                    sp.dma_start(out.rearrange("b t d -> (b t) d").rearrange("(j p) d -> p j d", p=TP)[p0:p1, js], h[p0:p1, js]).then_inc(stored, 16)
            sp.wait_ge(stored, 16 * 4 * 2)

        @block.scalar
        def _(act):
            act.dma_start(ident[:, :], a["ident"]).then_inc(ld_txt, 16)
            txt = a["txt"]
            with nc.allow_non_contiguous_dma(reason="rows of 768 bytes"):
                act.dma_start(h[64:94, 0::3, :], txt[0::2, 0:30, :].rearrange("b t d -> t b d")).then_inc(ld_txt, 16)
                act.dma_start(h[0:47, 1::3, :], txt[0::2, 30:77, :].rearrange("b t d -> t b d")).then_inc(ld_txt, 16)
                act.dma_start(h[17:94, 2::3, :], txt[1::2, :, :].rearrange("b t d -> t b d")).then_inc(ld_txt, 16)

            def root(n, rows, j0, count):
                act.wait_ge(ln_in, n)
                nc.scalar.activation(rstd[0:rows, j0:j0 + count], rstd[0:rows, j0:j0 + count], ACT.Sqrt).then_inc(ln_sqrt, 1)

            def copy_u(it, tiles):
                for m in tiles:
                    act.wait_ge(u_mm, MD * it + m + 1)
                    if m < CP:
                        need(act, conv_mm, CP * (it - 1) + m + 1)
                    else:
                        need(act, conv_d, it)
                    nc.scalar.activation(
                        upad[:, m, :, 3:3 + L].rearrange("p (a b) t -> p a b t", a=2),
                        pg[:, m % 2, :, 0:HG].rearrange("p a (b t) -> p a b t", b=2), ACT.Copy).then_inc(u_cp, 1)

            def first_tap(it, s, d):
                m, o = CP, 0 if d == 0 else 6
                need(act, op_mm, 2 * (it - 1))
                act.wait_ge(u_cp, MD * (it + 1))
                nc.scalar.activation(us[:, s, m, :].rearrange("p (b t) -> p b t", b=GB), upad[:, m, :, o:o + L], ACT.Identity,
                                     bias=chan[:, d, 0, m:m + 1], scale=conv_w[:, d, m, 0:1]).then_inc(tap_act, 1)

            def conv_taps(it, d):
                need(act, conv_mm, CP * it)
                for m in range(CP):
                    for k in range(4):
                        last = nc.scalar.activation(diag_conv[:, m, k, :], ident[:, :], ACT.Copy, scale=conv_w[:, d, m, k:k + 1])
                last.then_inc(taps_rdy, 1)

            def silu_u(it, s, d):
                for m in range(CP):
                    act.wait_ge(conv_mm, CP * it + m + 1)
                    nc.scalar.activation(us[:, s, m, :].rearrange("p (a n) -> p a n", a=2), pg[:, (m + 1) % 2, :, 0:HG],
                                         ACT.Silu, bias=chan[:, d, 0, m:m + 1]).then_inc(us_rdy, 1)
                act.wait_ge(conv_d, it + 1)
                nc.scalar.activation(us[:, s, CP, :], us[:, s, CP, :], ACT.Silu).then_inc(us_rdy, 1)

            def silu_z(it, s, tiles):
                for m in tiles:
                    act.wait_ge(z_mm, MD * it + m + 1)
                    if m == 0:
                        need(act, y_part, 6 * (it - 1))
                    nc.scalar.activation(sz[:, s, m, :].rearrange("p (a n) -> p a n", a=2),
                                         pg[:, Z_SLOT[m], :, 0:HG], ACT.Silu).then_inc(sz_rdy, 1)

            def first_silu_z(m, src):
                act.wait_ge(z_mm, m + 1)
                nc.scalar.activation(sz[:, 0, m, :].rearrange("p (a n) -> p a n", a=2), src[:, :, 0:HG], ACT.Silu).then_inc(sz_rdy, 1)

            def copy_dbl(it):
                act.wait_ge(xp_mm, it + 1)
                need(act, dt_mm, MD * it)
                need(act, bc_st, 16 * it)
                nc.scalar.activation(dbl[0:XP, :].rearrange("p (a n) -> p a n", a=2),
                                     pg[0:XP, 0, :, 0:HG], ACT.Copy).then_inc(dbl_rdy, 1)

            def abs_relu(it, s, d, tiles):
                for m in tiles:
                    act.wait_ge(dt_mm, MD * it + m + 1)
                    if m == 0:
                        need(act, du_d, MD * (it - 1))
                        need(act, dA_rdy, KI * (it - 1))
                        need(act, dbu_d, KI * (it - 1))
                    for dst, f in ((delta, ACT.Abs), (du, ACT.Relu)):
                        last = nc.scalar.activation(dst[:, s, m, :].rearrange("p (a n) -> p a n", a=2),
                                                    pg[:, (m + 1) % 2, :, 0:HG], f, bias=chan[:, d, 1, m:m + 1])
                    last.then_inc(x_cp, 1)

            def softplus(it, s):
                act.wait_ge(x_cp, MD * (it + 1))
                nc.scalar.activation(delta[:, s], delta[:, s], ACT.Exp, scale=-1.0).then_inc(exp_d, 1)
                act.wait_ge(exp_d, it + 1)
                nc.scalar.activation(delta[:, s], delta[:, s], ACT.Ln, bias=1.0).then_inc(sp_rdy, 1)

            def decay(it, s, d, k):
                c, m = k // MD, k % MD
                if k < MD:
                    act.wait_ge(delta_d, MD * it + m + 1)
                need(act, scan_d, KI * it + k - 1)
                rows = dA[:, k % 2, :].rearrange("p (n b t) -> p n b t", n=CN, b=GB)
                src = delta[:, s, m, :].rearrange("p (b t) -> p b t", b=GB)
                t0, t1 = (1, L) if d == 0 else (0, L - 1)
                for n in range(CN):
                    last = nc.scalar.activation(rows[:, n, :, t0:t1], src[:, :, t0:t1], ACT.Exp,
                                                scale=negA[:, d, m, CN * c + n:CN * c + n + 1])
                last.then_inc(dA_rdy, 1)

            def group(g, last):
                for d in range(2):
                    it = 2 * g + d
                    more = d == 0 or not last
                    for k in range(KI):
                        decay(it, d, d, k)
                        if begins(it) and k == 1:
                            first_silu_z(1, pg[:, 0])
                            first_silu_z(2, pg[:, 1])
                        if not more:
                            if k == 3:
                                root(5, TP, 0, 3 * GTILES)
                            if k in (6, 7, 8):
                                copy_xa(2 * (k - 6))
                                copy_xa(2 * (k - 6) + 1)
                            if k in (9, 11):
                                for n in range(2) if k == 9 else (2,):
                                    relu_router(n)
                        if more and k == 2:
                            copy_u(it + 1, (0, 1))
                        if more and k == 3:
                            copy_u(it + 1, (2,))
                        if more and k == 4:
                            first_tap(it + 1, 1 - d, 1 - d)
                            conv_taps(it + 1, 1 - d)
                        if more and k == 6:
                            silu_z(it + 1, 1 - d, (0, 1))
                        if more and k == 7:
                            silu_u(it + 1, 1 - d, 1 - d)
                        if more and k == 8:
                            copy_dbl(it + 1)
                        if more and k == 10:
                            abs_relu(it + 1, 1 - d, 1 - d, (0, 1))
                        if more and k == 11:
                            abs_relu(it + 1, 1 - d, 1 - d, (2,))
                            softplus(it + 1, 1 - d)
                            silu_z(it + 1, 1 - d, (2,))

            def copy_xa(n):
                act.wait_ge(xa_tr, n + 1)
                nc.scalar.activation(xT[0:KD, :, HG * n:HG * (n + 1)], pg[0:KD, n % 2, :, 0:HG], ACT.Copy).then_inc(xa_cp, 1)

            def relu_router(n):
                if n == 0:
                    act.wait_ge(ld_r, 16 * 4)
                act.wait_ge(r_mm, n + 1)
                need(act, s_mm, n - 1)
                for c in range(2):
                    last = nc.scalar.activation(hr[0:KD, n % 2, c, :], pg[0:KD, n % 2, c, 0:HG], ACT.Relu, bias=br1[0:KD, c:c + 1])
                last.then_inc(r_act, 1)

            root(1, 128, NT - ET, 2)
            root(2, TP, 0, GTILES)
            for s in range(2):
                act.wait_ge(ln_tr, s + 1)
                nc.scalar.activation(xT[0:KD, :, s * HG:(s + 1) * HG], py[0:KD, 2 * s:2 * s + 2, 0:HG], ACT.Copy).then_inc(ln_cp_act, 1)
            act.wait_ge(ld_txt, 64)
            act.wait_ge(ld_w, 16 * 14)
            conv_taps(0, 0)
            root(3, 128, NT - ET + 2, ET - 2)
            copy_u(0, (0, 1))
            nc.scalar.activation(negA[:, :, :, :], negA[:, :, :, :], ACT.Exp).then_inc(aexp, 1)
            copy_u(0, (2,))
            first_tap(0, 0, 0)
            silu_u(0, 0, 0)
            first_silu_z(0, py[:, 0:2])
            root(4, TP, GTILES, NT - GTILES)
            copy_dbl(0)
            abs_relu(0, 0, 0, range(MD))
            softplus(0, 0)
            act.wait_ge(aneg, 1)
            group(0, False)
            with act.Fori(1, NG - 1) as g:
                group(g, False)
            group(NG - 1, True)

            relu_router(3)
            root(6, TP, 3 * GTILES, GTILES)
            relu_router(4)
            relu_router(5)
            for n in (6, 7):
                copy_xa(n)
            for n in (6, 7):
                relu_router(n)
            act.wait_ge(top_in, 1)
            nc.scalar.activation(gate[0:TP], gate[0:TP], ACT.Exp).then_inc(r_exp, 1)

            def relu_tile(t, s):
                for bank, fs in ((0, range(0, FM // 2)), (1, range(FM // 2, FM))):
                    act.wait_ge(m_mm, 2 * t + bank + 1)
                    for f in fs:
                        last = nc.scalar.activation(mid[:, s % 2, f, :], pg[:, s % 2, bank, ST * (f - fs[0]):ST * (f - fs[0] + 1)], ACT.Relu,
                                                    bias=w2[s % 2][:, FM * D + f:FM * D + f + 1])
                    last.then_inc(m_act, 1)

            with act.Fori(0, BODIES) as i:
                for s in range(UN):
                    relu_tile(i * UN + s, s)
            for s in range(REST):
                relu_tile(BODIES * UN + s, s)
            for s in range(UN):
                act.wait_ge(ye_st[s], 16 * uses(s))
            for q in range(4):
                for p0, p1 in PARTS:
                    act.dma_start(yq[q][p0:p1, 1], ys[1 + TOK:1 + 2 * TOK, :].rearrange("(j p) d -> p j d", p=TP)
                                  [p0:p1, QT * q:QT * (q + 1)]).then_inc(ld_y[q][1], 16)
            act.wait_ge(share_rdy, 1)
            for q in range(4):
                act.wait_ge(ld_y[q][1], 16 * 2)
                for j in range(QT):
                    y1 = yq[q][0:TP, 1, j, :]
                    last = nc.scalar.activation(y1, y1, ACT.Copy, scale=share[0:TP, 1, QT * q + j:QT * q + j + 1])
                last.then_inc(scaled, 1)

        @block.tensor
        def _(pe):
            def transposes(n):
                pe.wait_ge(ln_xn, n + 1)
                for c in range(2):
                    for j in range(3):
                        last = nc.tensor.transpose(py[0:KD, 2 * (n % 2) + c, TP * j:TP * (j + 1)],
                                                   xn[0:TP, 3 * n + j, KD * c:KD * (c + 1)], ident[0:TP, 0:TP])
                last.then_inc(ln_tr, 1)

            for j in range(ET):
                if j == 0:
                    pe.wait_ge(ld_patch[0], 32)
                if j == 2:
                    pe.wait_ge(ld_patch[1], 16)
                if j == ET - 1:
                    pe.wait_ge(ld_txt, 64)
                    for n in range(2):
                        transposes(n)
                need(pe, emb_st, j - 1)
                for c in range(PK):
                    last = nc.tensor.matmul(pg[:, j % 2, 0, 0:D], patches[:, c, 128 * j:128 * (j + 1)], proj_w[:, c, :],
                                            start=(c == 0), stop=(c == PK - 1))
                last.then_inc(emb_mm, 1)

            pe.wait_ge(ln_cp_act, 2)
            pe.wait_ge(emb_st, ET)
            pe.wait_ge(ld_w, 16 * 14)

            def in_proj(g, d, m, dst):
                apart(pe)
                for half in range(2):
                    for c in range(2):
                        last = nc.tensor.matmul(dst[:, half, 0:HG], in_w[0:KD, d, c, 128 * m:128 * (m + 1)],
                                                xT[0:KD, c, bass.ds(g * GT + half * HG, HG)],
                                                start=(c == 0), stop=(c == 1))
                return last

            def proj_u(g, d, m):
                it = 2 * g + d
                if m == 0:
                    need(pe, sz_rdy, MD * it)
                if m == 1:
                    need(pe, x_cp, MD * it)
                if m == 2:
                    pe.wait_ge(u_cp, MD * it + 1)
                in_proj(g, d, m, pg[:, m % 2]).then_inc(u_mm, 1)

            def proj_z(g, d, m):
                it = 2 * g + d
                if m == 0:
                    pe.wait_ge(u_cp, MD * it + 2)
                    need(pe, h_add, 2 * (it - 1) - 1)
                if m == 1:
                    pe.wait_ge(u_cp, MD * it + 3)
                    need(pe, h_add, 2 * (it - 1))
                if m == 2:
                    pe.wait_ge(x_cp, MD * it + 2)
                in_proj(g, d, MD + m, pg[:, Z_SLOT[m]]).then_inc(z_mm, 1)

            def conv(it, d):
                pe.wait_ge(taps_rdy, it + 1)
                for m in range(CP):
                    if begins(it):
                        pe.wait_ge(u_cp, m + 2)
                    else:
                        pe.wait_ge(sz_rdy, MD * it + m + 1)
                    for half in range(2):
                        for k in range(4):
                            o = k if d == 0 else 6 - k
                            last = nc.tensor.matmul(pg[:, (m + 1) % 2, half, 0:HG], diag_conv[:, m, k, :],
                                                    upad[:, m, 2 * half:2 * half + 2, o:o + L], start=(k == 0), stop=(k == 3))
                    last.then_inc(conv_mm, 1)

            def xproj(g, d):
                it = 2 * g + d
                pe.wait_ge(us_rdy, MD * (it + 1))
                for half in range(2):
                    for m in range(MD):
                        last = nc.tensor.matmul(pg[0:XP, 0, half, 0:HG], xp_w[:, d, m, :],
                                                us[:, d, m, half * HG:(half + 1) * HG],
                                                start=(m == 0), stop=(m == MD - 1))
                last.then_inc(xp_mm, 1)

            def dt_proj(g, d, m):
                it = 2 * g + d
                if m == 0:
                    pe.wait_ge(dbl_rdy, it + 1)
                    pe.wait_ge(us_rdy, MD * it + 1)
                if m == 2:
                    pe.wait_ge(x_cp, MD * it + 1)
                for half in range(2):
                    last = nc.tensor.matmul(pg[:, (m + 1) % 2, half, 0:HG], dt_w[0:RANK, d, 128 * m:128 * (m + 1)],
                                            dbl[0:RANK, half * HG:(half + 1) * HG], start=True, stop=True)
                last.then_inc(dt_mm, 1)

            def out_proj(it, d, part):
                tiles = (range(0, 4), range(4, GTILES))[part]
                if part == 0:
                    pe.wait_ge(y_part, 6 * (it + 1))
                for j in tiles:
                    o = j - tiles[0]
                    for m in range(MD):
                        last = nc.tensor.matmul(pg[0:TP, 1 - part, o // 2, D * (o % 2):D * (o % 2) + D],
                                                us[:, d, m, TP * j:TP * (j + 1)], out_w[:, d, m, :],
                                                start=(m == 0), stop=(m == MD - 1))
                last.then_inc(op_mm, 1)

            def sum_states(it, d, k):
                c, m = k // MD, k % MD
                first_in_bank = {0: (True, True), 1: (False, True), 2: (False, True)}[m]
                if c == 0:
                    need(pe, y_part, 6 * (it - 1) + (3, 5, 6)[m])
                    for (bank, col, tok, w), fresh in zip(y_pieces(m), first_in_bank):
                        nc.tensor.matmul(py[:, bank, col:col + w], diagD[:, d, m, :], us[:, d, m, tok:tok + w],
                                         start=fresh, stop=False, skip_group_check=True)
                pe.wait_ge(hc_vec, KI * it + k + 1)
                for n in range(CN):
                    if k in POOL_STEPS and n == CN - PN:
                        pe.wait_ge(hc_pool, by_pool(it, k))
                    for bank, col, tok, w in y_pieces(m):
                        last = nc.tensor.matmul(py[:, bank, col:col + w], ident[:, :],
                                                X[:, k % 3, n * GT + tok:n * GT + tok + w],
                                                start=False, stop=(c == NC - 1 and n == CN - 1),
                                                skip_group_check=True)
                last.then_inc(y_mm, 1)

            def turn_xa(n):
                if n < 2:
                    pe.wait_ge(h_add, 2 * (2 * NG - 1))
                else:
                    pe.wait_ge(xa_cp, n - 1)
                pe.wait_ge(xa_rdy, 3 * n + 3)
                for c in range(2):
                    for j in range(3):
                        last = nc.tensor.transpose(pg[0:KD, n % 2, c, TP * j:TP * (j + 1)],
                                                   xa[3 * n + j][0:TP, KD * c:KD * (c + 1)], ident[0:TP, 0:TP])
                last.then_inc(xa_tr, 1)

            def router(n):
                if n == 0:
                    pe.wait_ge(ld_r, 16 * 4)
                pe.wait_ge(xa_cp, 6 if n < 2 else n + 1)
                for c in range(2):
                    for k in range(2):
                        last = nc.tensor.matmul(pg[0:KD, n % 2, c, 0:HG], wr1[0:KD, k, KD * c:KD * (c + 1)],
                                                xT[0:KD, k, HG * n:HG * (n + 1)], start=(k == 0), stop=(k == 1))
                last.then_inc(r_mm, 1)

            def scores(n):
                pe.wait_ge(r_act, n + 1)
                for j in range(3):
                    o = 2 * D + NE * (3 * (n // 2) + j)
                    for c in range(2):
                        last = nc.tensor.matmul(pg[0:TP, n % 2, 0, o:o + NE], hr[0:KD, n % 2, c, TP * j:TP * (j + 1)],
                                                wr2[0:KD, c, :], start=(c == 0), stop=(c == 1))
                last.then_inc(s_mm, 1)

            def group(g, first, last):
                for d in range(2):
                    it = 2 * g + d
                    more = d == 0 or not last
                    prev = d == 1 or not first
                    n = (g, 1) if d == 0 else (g + 1, 0)
                    for k in range(KI):
                        if not more:
                            if k in (5, 6, 7):
                                turn_xa(2 * (k - 5))
                                turn_xa(2 * (k - 5) + 1)
                            if k == 8:
                                router(0)
                                router(1)
                        if more:
                            if k == 0:
                                proj_u(*n, 0)
                                proj_u(*n, 1)
                            if k == 1:
                                proj_u(*n, 2)
                        if prev and k == 2:
                            if more:
                                pe.wait_ge(u_cp, MD * (it + 1) + 2)
                            else:
                                pe.wait_ge(x_cp, MD * (it + 1))
                                pe.wait_ge(sz_rdy, MD * (it + 1))
                            out_proj(it - 1, 1 - d, 0)
                            if more:
                                pe.wait_ge(u_cp, MD * (it + 1) + 3)
                            out_proj(it - 1, 1 - d, 1)
                        if more:
                            if k == 4:
                                proj_z(*n, 0)
                                proj_z(*n, 1)
                            if k == 5:
                                conv(it + 1, 1 - d)
                            if k == 6:
                                xproj(*n)
                            if k == 8:
                                dt_proj(*n, 0)
                                dt_proj(*n, 1)
                            if k == 9:
                                dt_proj(*n, 2)
                            if k == 10:
                                proj_z(*n, 2)
                        sum_states(it, d, k)
                        if not more and k == 9:
                            scores(0)
                            router(2)

            for m in range(MD):
                proj_u(0, 0, m)
            conv(0, 0)
            in_proj(0, 0, MD, py[:, 0:2]).then_inc(z_mm, 1)
            xproj(0, 0)
            for m in range(MD):
                dt_proj(0, 0, m)
            pe.wait_ge(sz_rdy, 1)
            for n in range(2, 2 * NG):
                need(pe, ln_cp_vec, n - 3)
                transposes(n)
            pe.wait_ge(ln_cp_vec, 2 * NG - 2)
            pe.wait_ge(x_cp, MD)
            for m in (1, 2):
                in_proj(0, 0, MD + m, pg[:, m - 1]).then_inc(z_mm, 1)
            pe.wait_ge(diag_rdy, 1)
            group(0, True, False)
            with pe.Fori(1, NG - 1) as g:
                group(g, False, False)
            group(NG - 1, False, True)
            scores(1)
            scores(2)
            pe.wait_ge(s_cp, 2)
            out_proj(2 * NG - 1, 1, 0)
            out_proj(2 * NG - 1, 1, 1)
            pe.wait_ge(h_add, 4 * NG)
            router(3)
            router(4)
            scores(3)
            router(5)
            scores(4)
            scores(5)
            for n in (6, 7):
                turn_xa(n)
            for n in (6, 7):
                router(n)
            for n in (6, 7):
                scores(n)
            pe.wait_ge(ld_c, 16 * 5)
            pe.wait_ge(pos_rdy, 1)
            for b in range(2):
                last = nc.tensor.matmul(py[0:TP, b, 0:NT * NE], tri[0:TP, b, :], chosen[0:TP].rearrange("p j e -> p (j e)"),
                                        start=True, stop=True)
            last.then_inc(cnt_mm, 1)
            for n in range(2 * NT):
                if n % (NT // 2) == 0:
                    if n // (NT // 2) < 3:
                        pe.wait_ge(hot_pool, n // (NT // 2) + 1)
                    else:
                        pe.wait_ge(hot, 4 + 1)
                last = nc.tensor.matmul(py[:, 2, 0:2 * ETILES], is_row[0:TP, n, :], id_tile[0:TP, :, n, :],
                                        start=(n == 0), stop=(n == 2 * NT - 1))
            last.then_inc(id_mm, 1)
            pe.wait_ge(idx_rdy, 1)

            def turn_rows(i, s):
                pe.wait_ge(ld_x[s], 16 * (i + 1))
                for c in range(2):
                    last = nc.tensor.transpose(py[0:KD, s % 2, ST * c:ST * (c + 1)], xg[:, s, KD * c:KD * (c + 1)], ident[:, :])
                last.then_inc(xg_tr, 1)

            def second_layer(t, s):
                for f in range(FM):
                    if f == 0:
                        pe.wait_ge(m_act, 2 * t + 1)
                    if f == FM // 2:
                        pe.wait_ge(m_act, 2 * t + 2)
                    last = nc.tensor.matmul(py[:, 2 + s % 2, 0:D], mid[:, s % 2, f, :], w2[s % 2][:, D * f:D * (f + 1)],
                                            start=(f == 0), stop=(f == FM - 1))
                last.then_inc(e_mm, 1)

            def first_layer(t, s):
                pe.wait_ge(xg_cp, t + 1)
                pe.wait_ge(w_rdy, t + 1)
                for f in range(FM):
                    for c in range(2):
                        last = nc.tensor.matmul(pg[:, s % 2, 2 * f // FM, ST * (f % (FM // 2)):ST * (f % (FM // 2) + 1)],
                                                w1[s % 2][0:KD, c, 128 * f:128 * (f + 1)], xgT[0:KD, s % 2, c, :],
                                                start=(c == 0), stop=(c == 1))
                    if f in (FM // 2 - 1, FM - 1):
                        last.then_inc(m_mm, 1)

            def tiles(i, first, count=UN):
                for s in range(count):
                    t = i * UN + s
                    turn_rows(i, s)
                    if not (first and s == 0):
                        need(pe, ye_cp, t - 2)
                        second_layer(t - 1, (s - 1) % UN)
                    first_layer(t, s)

            tiles(0, True)
            with pe.Fori(1, BODIES) as i:
                tiles(i, False)
            tiles(BODIES, False, REST)
            second_layer(ETILES - 1, REST - 1)

        @block.vector
        def _(dve):
            chain = [0]

            def then_next(ins):
                chain[0] += 1
                ins.then_inc(ln_chain, 1)
                dve.wait_ge(ln_chain, chain[0])

            nc.vector.memset(zeros[:, :], 0.0).then_inc(zero_d, 1)
            then_next(nc.vector.memset(upad[:, :, :, :], 0.0))

            def moments(rows, j0, count):
                js = slice(j0, j0 + count)
                st = stats[0:rows, js, :]
                s0, s1, s2 = (lnt[0:rows, i, 0:count] for i in range(3))
                then_next(nc.vector.tensor_tensor(s0, st[:, :, 1], st[:, :, 4], ALU.add))
                then_next(nc.vector.tensor_tensor(s1, st[:, :, 1], st[:, :, 4], ALU.subtract))
                then_next(nc.vector.tensor_tensor(s2, st[:, :, 2], st[:, :, 5], ALU.add))
                then_next(nc.vector.tensor_scalar(mean[0:rows, js], s0, 0.5, None, ALU.mult))
                then_next(nc.vector.scalar_tensor_tensor(s1, s1, 0.25, s1, ALU.mult, ALU.mult))
                then_next(nc.vector.scalar_tensor_tensor(s2, s2, 1.0 / D, s1, ALU.mult, ALU.add))
                nc.vector.tensor_scalar(rstd[0:rows, js], s2, EPS, None, ALU.add).then_inc(ln_in, 1)

            def reciprocal_root(n, rows, j0, count):
                js = slice(j0, j0 + count)
                dve.wait_ge(ln_sqrt, n)
                then_next(nc.vector.reciprocal(rstd[0:rows, js], rstd[0:rows, js]))

            def embed(tiles):
                for j in tiles:
                    dve.wait_ge(emb_mm, j + 1)
                    nc.vector.tensor_tensor(emb[:, j, :], pg[:, j % 2, 0, 0:D], embrow[:, 0, :], ALU.add).then_inc(emb_st, 1)
                    dve.wait_ge(emb_st, j + 1)
                    last = nc.vector.bn_stats(stats[:, NT - ET + j, :], emb[:, j, :])
                then_next(last)

            def embed_norm(n, j0, j1):
                moments(128, NT - ET + j0, j1 - j0)
                reciprocal_root(n, 128, NT - ET + j0, j1 - j0)
                for j in range(j0, j1):
                    o = NT - ET + j
                    last = nc.vector.tensor_scalar(emb[:, j, :], emb[:, j, :], mean[:, o:o + 1], rstd[:, o:o + 1],
                                                   ALU.subtract, ALU.mult)
                then_next(last)
                row = lambda r: embrow[:, r, :].unsqueeze(1).to_broadcast([128, j1 - j0, D])
                then_next(nc.vector.tensor_tensor(emb[:, j0:j1, :], emb[:, j0:j1, :], row(1), ALU.mult))
                nc.vector.tensor_tensor(emb[:, j0:j1, :], emb[:, j0:j1, :], row(2), ALU.add).then_inc(emb_dn, 1)

            def statistics(j0, j1):
                for j in range(j0, j1):
                    last = nc.vector.bn_stats(stats[0:TP, j, :], h[0:TP, j, :])
                then_next(last)
                moments(TP, j0, j1 - j0)

            def normalise(j0, j1):
                for j in range(j0, j1):
                    last = nc.vector.tensor_scalar(xn[0:TP, j, :], h[0:TP, j, :], mean[0:TP, j:j + 1], rstd[0:TP, j:j + 1],
                                                   ALU.subtract, ALU.mult)
                    if j % 3 == 2:
                        last.then_inc(ln_xn, 1)

            dve.wait_ge(ld_emb, 48)
            embed(range(0, 2))
            embed_norm(1, 0, 2)
            embed(range(2, 5))
            dve.wait_ge(ld_txt, 64)
            dve.wait_ge(emb_h[0], 16 * 5)
            statistics(0, GTILES)
            reciprocal_root(2, TP, 0, GTILES)
            normalise(0, GTILES)
            embed(range(5, ET))
            embed_norm(3, 2, ET)
            dve.wait_ge(aexp, 1)
            nc.vector.tensor_scalar(negA[:, :, :, :], negA[:, :, :, :], -1.0, None, ALU.mult).then_inc(aneg, 1)
            for d in range(2):
                for m in range(MD):
                    last = nc.vector.tensor_scalar(diagD[:, d, m, :], ident[:, :], chan[:, d, 2, m:m + 1], None, ALU.mult)
            last.then_inc(diag_rdy, 1)

            def conv(it, s, d):
                m = CP
                dve.wait_ge(tap_act, it + 1)
                dst = us[:, s, m, :].rearrange("p (b t) -> p b t", b=GB)
                for k in range(1, 4):
                    o = k if d == 0 else 6 - k
                    if k > 1:
                        dve.wait_ge(tap_d, 2 * it + k - 1)
                    nc.vector.scalar_tensor_tensor(dst, upad[:, m, :, o:o + L], conv_w[:, d, m, k:k + 1], dst, ALU.mult, ALU.add)\
                        .then_inc(conv_d if k == 3 else tap_d, 1)

            by_state = lambda x: x.rearrange("p (n t) -> p n t", n=CN)

            def mult_b(it, s, k):
                c, m = k // MD, k % MD
                if k < MD:
                    dve.wait_ge(du_d, MD * it + m + 1)
                if m == 0:
                    dve.wait_ge(bc_ld[c % 2], 64 * it + 32 * (c // 2) + 32)
                need(dve, y_mm, KI * it + k - 2)
                nc.vector.tensor_tensor(by_state(X[:, k % 3, :]), du[:, s, m, :].unsqueeze(1).to_broadcast([128, CN, GT]),
                                        by_state(bc[:, c % 2, 0, :]), ALU.mult).then_inc(dbu_d, 1)

            def scan(it, d, k):
                if k < 2:
                    t0 = 0 if d == 0 else L - 1
                    need(dve, scan_d, KI * it + k - 1)
                    nc.vector.memset(dA[:, k % 2, :].rearrange("p (r t) -> p r t", t=L)[:, :, t0:t0 + 1], 0.0).then_inc(zero_col, 1)
                    dve.wait_ge(zero_col, 2 * it + k + 1)
                dve.wait_ge(dA_rdy, KI * it + k + 1)
                dve.wait_ge(dbu_d, KI * it + k + 1)
                x, dec = X[:, k % 3, :], dA[:, k % 2, :]
                if d == 1:
                    x, dec = x[:, ::-1], dec[:, ::-1]
                nc.vector.tensor_tensor_scan(x, dec, x, 0.0, ALU.mult, ALU.add).then_inc(scan_d, 1)

            def mult_c(it, k):
                w = (CN - PN if k in POOL_STEPS else CN) * GT
                x = X[:, k % 3, 0:w]
                dve.wait_ge(scan_d, KI * it + k + 1)
                nc.vector.tensor_tensor(x, x, bc[:, k // MD % 2, 1, 0:w], ALU.mult).then_inc(hc_vec, 1)

            def finish(it, s, d):
                dve.wait_ge(y_mm, KI * (it + 1))
                for m in range(MD):
                    for bank, col, tok, w in y_pieces(m):
                        nc.vector.tensor_tensor(us[:, s, m, tok:tok + w], py[:, bank, col:col + w],
                                                sz[:, s, m, tok:tok + w], ALU.mult).then_inc(y_part, 1)

            def add_out(g, it, part):
                tiles = (range(0, 4), range(4, GTILES))[part]
                n = len(tiles) // 2
                dve.wait_ge(op_mm, 2 * it + part + 1)
                need(dve, h_add, 2 * it + part)
                dst = h[0:TP, bass.ds(GTILES * g + tiles[0], 2 * n), :].rearrange("p (a b) d -> p a b d", a=n)
                nc.vector.tensor_tensor(dst, dst, pg[0:TP, 1 - part, 0:n, 0:2 * D].rearrange("p a (b d) -> p a b d", b=2),
                                        ALU.add).then_inc(h_add, 1)

            def normalise_xa(j0, j1):
                for j in range(j0, j1):
                    nc.vector.tensor_scalar(xa[j][0:TP, :], h[0:TP, j, :], mean[0:TP, j:j + 1], rstd[0:TP, j:j + 1],
                                            ALU.subtract, ALU.mult).then_inc(xa_rdy, 1)

            def group(g, first, last):
                for d in range(2):
                    it = 2 * g + d
                    more = d == 0 or not last
                    prev = d == 1 or not first
                    for k in range(KI):
                        if prev and k == 1:
                            finish(it - 1, 1 - d, 1 - d)
                        if prev and k == 4:
                            add_out(g - 1 if d == 0 else g, it - 1, 0)
                            add_out(g - 1 if d == 0 else g, it - 1, 1)
                        if not more and k == 2:
                            statistics(0, 3 * GTILES)
                        if not more and k == 3:
                            reciprocal_root(5, TP, 0, 3 * GTILES)
                            dve.wait_ge(dA_rdy, KI * it)
                            normalise_xa(0, 3 * GTILES)
                        if more and k == 5:
                            conv(it + 1, 1 - d, 1 - d)
                        if k == 0:
                            mult_b(it, d, 0)
                        scan(it, d, k)
                        if k + 1 < KI:
                            mult_b(it, d, k + 1)
                        mult_c(it, k)

            conv(0, 0, 0)
            dve.wait_ge(emb_h[1], 16 * 5)
            statistics(GTILES, NT)
            reciprocal_root(4, TP, GTILES, NT - GTILES)
            normalise(GTILES, NT)
            for n in range(2, 2 * NG):
                dve.wait_ge(ln_tr, n + 1)
                nc.vector.tensor_copy(xT[0:KD, :, n * HG:(n + 1) * HG], py[0:KD, 2 * (n % 2):2 * (n % 2) + 2, 0:HG]).then_inc(ln_cp_vec, 1)
            dve.wait_ge(sp_rdy, 1)
            nc.vector.tensor_tensor(delta[:, 0, 0], delta[:, 0, 0], du[:, 0, 0], ALU.add).then_inc(delta_d, 1)
            dve.wait_ge(delta_d, 1)
            nc.vector.tensor_tensor(du[:, 0, 0], delta[:, 0, 0], us[:, 0, 0], ALU.mult).then_inc(du_d, 1)
            group(0, True, False)
            with dve.Fori(1, NG - 1) as g:
                group(g, False, False)
            group(NG - 1, False, True)
            finish(2 * NG - 1, 1, 1)
            sc, rk, cm, gt, ps, cu, ct = (x[0:TP] for x in (score, chosen, tmp, gate, pos, cum, cnt))
            by_j = lambda x: x.unsqueeze(2).to_broadcast([TP, NT, NE])

            def copy_scores(s, q0, q1):
                nc.vector.tensor_tensor(score[0:TP].rearrange("p (q s j) e -> p s q j e", s=2, j=3)[:, s, q0:q1],
                                        pg[0:TP, s, 0, 2 * D:2 * D + NT // 2 * NE].rearrange("p (q j e) -> p q j e", q=NG, j=3)[:, q0:q1],
                                        br2[0:TP, :].unsqueeze(1).unsqueeze(1).to_broadcast([TP, q1 - q0, 3, NE]), ALU.add).then_inc(s_cp, 1)

            def ranks(j0, j1):
                n = j1 - j0
                for o in range(NE):
                    other = score[0:TP, j0:j1, o:o + 1]
                    last = nc.vector.tensor_tensor(above[0:TP, j0:j1, 0:o + 1, o], other.to_broadcast([TP, n, o + 1]), sc[:, j0:j1, 0:o + 1], ALU.is_gt)
                    if o < NE - 1:
                        last = nc.vector.tensor_tensor(above[0:TP, j0:j1, o + 1:NE, o], other.to_broadcast([TP, n, NE - 1 - o]), sc[:, j0:j1, o + 1:NE], ALU.is_ge)
                then_next(last)
                then_next(nc.vector.tensor_reduce(rk[:, j0:j1], above[0:TP, j0:j1], AX.X, ALU.add))

            dve.wait_ge(ld_r, 16 * 4)
            dve.wait_ge(s_mm, 3)
            copy_scores(0, 0, 2)
            copy_scores(1, 0, 1)
            dve.wait_ge(s_cp, 2)
            ranks(0, 9)
            add_out(NG - 1, 2 * NG - 1, 0)
            add_out(NG - 1, 2 * NG - 1, 1)
            dve.wait_ge(h_add, 4 * NG)

            statistics(3 * GTILES, NT)
            reciprocal_root(6, TP, 3 * GTILES, GTILES)
            normalise_xa(3 * GTILES, NT)
            dve.wait_ge(s_mm, 8)
            copy_scores(0, 2, 4)
            copy_scores(1, 1, 4)
            dve.wait_ge(s_cp, 4)
            ranks(9, NT)
            nc.vector.tensor_scalar(rk, rk, 1.5, None, ALU.is_lt).then_inc(pos_rdy, 1)
            then_next(nc.vector.tensor_reduce(rowmax[0:TP], sc, AX.X, ALU.max))
            nc.vector.tensor_tensor(gt, sc, by_j(rowmax[0:TP]), ALU.subtract).then_inc(top_in, 1)
            dve.wait_ge(pos_rdy, 1)
            dve.wait_ge(ld_c, 16 * 5)
            nc.vector.tensor_copy(iota_h[0:TP], iota[0:TP])
            nc.vector.tensor_copy(tstart_h[0:TP], tstart[0:TP, 0:ETILES])
            then_next(nc.vector.tensor_copy(ids_h[0:TP], ids[0:TP]))
            then_next(nc.vector.memset(ones_j[0:TP], 1.0))
            dve.wait_ge(cnt_mm, 1)
            nc.vector.tensor_copy(ps, py[0:TP, 0, 0:NT * NE].rearrange("p (j e) -> p j e", e=NE))
            then_next(nc.vector.tensor_copy(ct, py[0:TP, 1, 0:NT * NE].rearrange("p (j e) -> p j e", e=NE)))
            for e in range(NE):
                last = nc.vector.tensor_tensor_scan(cu[:, :, e], ones_j[0:TP], ct[:, :, e], 0.0, ALU.mult, ALU.add)
            then_next(last)
            then_next(nc.vector.tensor_tensor(ct, cu, ct, ALU.subtract))
            then_next(nc.vector.tensor_tensor(ps, ps, ct, ALU.add))
            then_next(nc.vector.tensor_scalar(counts[0:TP], cu[:, NT - 1, :], float(ST - 1), None, ALU.add))
            then_next(nc.vector.tensor_copy(padded_i[0:TP], counts[0:TP]))
            then_next(nc.vector.tensor_scalar(padded_i[0:TP], padded_i[0:TP], -ST, None, ALU.bitwise_and))
            then_next(nc.vector.tensor_copy(padded[0:TP], padded_i[0:TP]))
            then_next(nc.vector.tensor_tensor_scan(ends[0:TP], ones_j[0:TP, 0:NE], padded[0:TP], 0.0, ALU.mult, ALU.add))
            then_next(nc.vector.tensor_tensor(starts[0:TP], ends[0:TP], padded[0:TP], ALU.subtract))
            then_next(nc.vector.tensor_tensor(ps, ps, starts[0:TP].unsqueeze(1).to_broadcast([TP, NT, NE]), ALU.add))
            then_next(nc.vector.tensor_scalar(cm, rk, -FAR, FAR, ALU.mult, ALU.add))
            then_next(nc.vector.tensor_tensor(cm, cm, ps, ALU.add))
            then_next(nc.vector.tensor_reduce(where[0:TP, 0, :], cm, AX.X, ALU.min))
            then_next(nc.vector.tensor_tensor(cm, ps, rk, ALU.mult))
            then_next(nc.vector.tensor_reduce(where[0:TP, 1, :], cm, AX.X, ALU.max))
            then_next(nc.vector.tensor_copy(lo_i[0:TP], where[0:TP]))
            then_next(nc.vector.tensor_scalar(lo_i[0:TP], lo_i[0:TP], ST - 1, None, ALU.bitwise_and))
            then_next(nc.vector.tensor_copy(lo[0:TP], lo_i[0:TP]))
            then_next(nc.vector.tensor_tensor(base[0:TP], where[0:TP], lo[0:TP], ALU.subtract))
            dve.wait_ge(op_mm, 4 * NG)
            half = NT // 2
            for n in range(4):
                b, js = n // 2, slice(half * (n % 2), half * (n % 2 + 1))
                ns = slice(half * n, half * (n + 1))
                nc.vector.tensor_tensor(is_row[0:TP, ns, :], iota_h[0:TP].unsqueeze(1).to_broadcast([TP, half, ST]),
                                        lo[0:TP, b, js].unsqueeze(2).to_broadcast([TP, half, ST]), ALU.is_equal)
                nc.vector.tensor_tensor(is_tile[0:TP, ns, :], tstart_h[0:TP].unsqueeze(1).to_broadcast([TP, half, ETILES]),
                                        base[0:TP, b, js].unsqueeze(2).to_broadcast([TP, half, ETILES]), ALU.is_equal).then_inc(hot, 1)
            dve.wait_ge(hot, 4)
            number_tiles(nc.vector, 3).then_inc(hot, 1)
            ended = above.rearrange("p j e o -> p (j e o)")[0:1, 0:(ETILES + 1) * (NE - 1)].rearrange("p (t e) -> p t e", e=NE - 1)
            then_next(nc.vector.tensor_tensor(ended, tstart[0:1].unsqueeze(2).to_broadcast([1, ETILES + 1, NE - 1]),
                                              ends[0:1, 0:NE - 1].unsqueeze(1).to_broadcast([1, ETILES + 1, NE - 1]), ALU.is_ge))
            then_next(nc.vector.tensor_reduce(texp[0:1], ended, AX.X, ALU.add))
            nc.vector.tensor_copy(texp_i[0:1], texp[0:1]).then_inc(tab_rdy, 1)
            dve.wait_ge(id_mm, 1)
            then_next(nc.vector.tensor_scalar(row_to, py[:, 2, 0:ETILES], float(IDB), None, ALU.mult))
            then_next(nc.vector.tensor_tensor(row_from, py[:, 2, ETILES:2 * ETILES], row_to, ALU.add))
            then_next(nc.vector.scalar_tensor_tensor(row_to, row_from, 0.0, dump, ALU.is_equal, ALU.mult))
            then_next(nc.vector.tensor_tensor(row_to, row_to, row_from, ALU.add))
            then_next(nc.vector.tensor_copy(row_to_i, row_to))
            then_next(nc.vector.tensor_scalar(row_to, row_from, float(TOK), -float(TOK), ALU.is_gt, ALU.mult))
            then_next(nc.vector.tensor_tensor(row_from, row_from, row_to, ALU.add))
            nc.vector.tensor_copy(row_from_i, row_from).then_inc(idx_rdy, 1)
            dve.wait_ge(ld_home, 16 * 3 * NE)
            dve.wait_ge(xa_st, 16 * 9)
            dve.wait_ge(tab_rdy, 1)

            def gates(part):
                if part == 0:
                    dve.wait_ge(r_exp, 1)
                    then_next(nc.vector.tensor_tensor(gt, gt, rk, ALU.mult))
                    then_next(nc.vector.tensor_reduce(rowsum[0:TP], gt, AX.X, ALU.add))
                    then_next(nc.vector.reciprocal(rowsum[0:TP], rowsum[0:TP]))
                    then_next(nc.vector.tensor_tensor(gt, gt, by_j(rowsum[0:TP]), ALU.mult))
                else:
                    b = part - 1
                    then_next(nc.vector.tensor_tensor(cm, ps, by_j(where[0:TP, b, :]), ALU.is_equal))
                    then_next(nc.vector.tensor_tensor(cm, cm, gt, ALU.mult))
                    last = nc.vector.tensor_reduce(share[0:TP, b, :], cm, AX.X, ALU.add)
                    if b == 0:
                        then_next(last)
                    else:
                        last.then_inc(share_rdy, 1)

            def fetch(t, s):
                need(dve, ye_cp, t - 1)
                apart(dve)
                e = dve.value_load(texp_i[0:1, bass.ds(t, 1)], min_val=0, max_val=NE - 1)
                nc.vector.tensor_copy(w1[s % 2][0:KD].rearrange("p c f -> p (c f)"),
                                      home[0:KD, bass.ds(e, 1), 0:EW1].rearrange("p o f -> p (o f)"))
                nc.vector.tensor_copy(w2[s % 2], home[:, bass.ds(e, 1), EW1:].rearrange("p o f -> p (o f)")).then_inc(w_rdy, 1)

            def copy_rows(t, s):
                dve.wait_ge(xg_tr, t + 1)
                nc.vector.tensor_copy(xgT[0:KD, s % 2], py[0:KD, s % 2, 0:2 * ST].rearrange("p (c n) -> p c n", c=2)).then_inc(xg_cp, 1)

            def copy_out(i, t, s, first):
                dve.wait_ge(e_mm, t + 1)
                if not first:
                    dve.wait_ge(ye_st[s], 16 * i)
                nc.vector.tensor_tensor(ye[:, s], py[:, 2 + s % 2, 0:D], w2[s % 2][:, EW2:EW2 + D], ALU.add).then_inc(ye_cp, 1)

            def tiles(i, first, count=UN):
                for s in range(count):
                    copy_rows(i * UN + s, s)
                    if s > 0:
                        copy_out(i, i * UN + s - 1, s - 1, first)
                    elif not first:
                        copy_out(i - 1, i * UN - 1, UN - 1, isinstance(i, int) and i == 1)
                    if count == UN or s + 1 < count:
                        fetch(i * UN + s + 1, (s + 1) % UN)
                    if first and s > 0:
                        gates(s - 1)

            fetch(0, 0)
            tiles(0, True)
            tiles(1, False)
            with dve.Fori(2, BODIES) as i:
                tiles(i, False)
            tiles(BODIES, False, REST)
            copy_out(BODIES, ETILES - 1, REST - 1, False)
            def add_first(q):
                dve.wait_ge(ld_y[q][0], 16 * 2)
                for j in range(QT * q, QT * (q + 1)):
                    last = nc.vector.scalar_tensor_tensor(h[0:TP, j, :], yq[q][0:TP, 0, j - QT * q, :], share[0:TP, 0, j:j + 1],
                                                          h[0:TP, j, :], ALU.mult, ALU.add)
                last.then_inc(first_add, 1)

            def add_second(q):
                dve.wait_ge(first_add, q + 1)
                dve.wait_ge(scaled, q + 1)
                js = slice(QT * q, QT * (q + 1))
                nc.vector.tensor_tensor(h[0:TP, js, :], h[0:TP, js, :], yq[q][0:TP, 1], ALU.add).then_inc(moe_add, 1)

            for q in range(4):
                add_first(q)
                if q > 0:
                    add_second(q - 1)
            add_second(3)

        @block.gpsimd
        def _(pool):
            def softplus_sum(it, s, tiles=range(MD)):
                pool.wait_ge(sp_rdy, it + 1)
                pool.wait_ge(us_rdy, MD * (it + 1))
                for m in tiles:
                    nc.gpsimd.tensor_tensor(delta[:, s, m], delta[:, s, m], du[:, s, m], ALU.add).then_inc(delta_d, 1)
                    pool.wait_ge(delta_d, MD * it + m + 1)
                    nc.gpsimd.tensor_tensor(du[:, s, m], delta[:, s, m], us[:, s, m], ALU.mult).then_inc(du_d, 1)

            def group(g, last):
                for d in range(2):
                    it = 2 * g + d
                    for k in POOL_STEPS:
                        c = k // MD
                        pool.wait_ge(scan_d, KI * it + k + 1)
                        x = X[:, k % 3, (CN - PN) * GT:]
                        pool.wait_ge(bc_ld[c % 2], 64 * it + 32 * (c // 2) + 32)
                        nc.gpsimd.tensor_tensor(x, x, bc[:, c % 2, 1, (CN - PN) * GT:], ALU.mult).then_inc(hc_pool, 1)
                    if d == 0 or not last:
                        softplus_sum(it + 1, 1 - d)

            pool.wait_ge(du_d, 1)
            softplus_sum(0, 0, range(1, MD))
            group(0, False)
            with pool.Fori(1, NG - 1) as g:
                group(g, False)
            group(NG - 1, True)

            def gather(t, s):
                need(pool, xg_tr, t - UN + 1)
                apart(pool)
                nc.gpsimd.tensor_copy(from_now[:, s:s + 1], row_from_i[:, bass.ds(t, 1)]).then_inc(from_cp, 1)
                pool.wait_ge(from_cp, t + 1)
                apart(pool)
                pool.indirect_dma_start(xg[:, s], None, xr, bass.IndirectOffsetOnAxis(from_now[:, s:s + 1], 0)).then_inc(ld_x[s], 16)

            def scatter(t, s):
                pool.wait_ge(ye_cp, t + 1)
                apart(pool)
                nc.gpsimd.tensor_copy(to_now[:, s:s + 1], row_to_i[:, bass.ds(t, 1)]).then_inc(to_cp, 1)
                pool.wait_ge(to_cp, t + 1)
                apart(pool)
                pool.indirect_dma_start(ys, bass.IndirectOffsetOnAxis(to_now[:, s:s + 1], 0), ye[:, s], None).then_inc(ye_st[s], 16)

            def tiles(i):
                for s in range(UN):
                    gather(i * UN + s + UN - 1, (s + UN - 1) % UN)
                    scatter(i * UN + s, s)

            for n in range(3):
                pool.wait_ge(hot, n + 1)
                number_tiles(nc.gpsimd, n).then_inc(hot_pool, 1)
            pool.wait_ge(xa_st, 16 * 9)
            pool.wait_ge(idx_rdy, 1)
            for s in range(UN - 1):
                gather(s, s)
            assert REST == UN - 1
            tiles(0)
            with pool.Fori(1, BODIES) as i:
                tiles(i)
            for s in range(REST):
                scatter(BODIES * UN + s, s)


def kernel(**inputs):
    import concourse.bacc as bacc
    from concourse.bass_utils import run_bass_kernel_spmd

    v = {n: np.asarray(x) for n, x in inputs.items()}
    P = PATCH
    x = v["x"]
    hp, wp = x.shape[2] // P, x.shape[3] // P
    host = {
        "patches": x.reshape(BATCH, 3, hp, P, wp, P).transpose(1, 3, 5, 0, 2, 4).reshape(3 * P * P, BATCH * hp * wp),
        "txt": v["txt"], "proj_wT": v["L0_tok_W_proj"].T, "proj_b": v["L0_tok_b_proj"],
        "gamma": v["L0_tok_gamma"], "beta": v["L0_tok_beta"],
        "W1T": v["L0_ffn_W1"].transpose(0, 2, 1),
        "W2b1": np.concatenate([v["L0_ffn_W2"].transpose(0, 2, 1).reshape(NE, FM, 128, D).transpose(0, 2, 1, 3).reshape(NE, 128, FM * D),
                                v["L0_ffn_b1"].reshape(NE, FM, 128).transpose(0, 2, 1)], axis=2),
        "tri": np.stack([np.triu(np.ones((TP, TP), np.float32), 1), np.ones((TP, TP), np.float32)], axis=1),
        "tstart": np.arange(0, (ETILES + 1) * ST, ST, dtype=np.float32), "iota": np.arange(ST, dtype=np.float32),
        "ids": np.stack(np.divmod(1 + np.arange(2 * TOK), IDB)).astype(np.float32).reshape(2, 2 * NT, TP).transpose(2, 0, 1),
        "dump": (ER + np.arange(ETILES * ST, dtype=np.float32)).reshape(ETILES, ST).T,
        "b2": v["L0_ffn_b2"], "Wr1T": v["L0_ffn_Wr1"].T, "br1": v["L0_ffn_br1"],
        "Wr2T": v["L0_ffn_Wr2"].T, "br2": v["L0_ffn_br2"], "ident": np.eye(128, dtype=np.float32),
    }
    for p in "fb":
        w = {n: v[f"L0_attn_{p}_{n}"] for n in ("in_w", "conv_w", "conv_b", "xproj_w", "dt_w", "dt_b", "Alog", "D", "out_w")}
        host.update({p + "_in_wT": w["in_w"].T, p + "_xproj_wT": w["xproj_w"].T, p + "_dt_wT": w["dt_w"].T,
                     p + "_out_wT": w["out_w"].T, p + "_conv_w": w["conv_w"], p + "_Alog": w["Alog"],
                     p + "_chan": np.stack([w[n].reshape(MD, 128).T for n in ("conv_b", "dt_b", "D")], axis=1)})
    nc = bacc.Bacc("TRN2", target_bir_lowering=False, num_devices=1)
    arrays, aps = {}, {}
    for n, arr in host.items():
        arrays["in_" + n] = np.ascontiguousarray(arr)
        aps[n] = nc.dram_tensor("in_" + n, arrays["in_" + n].shape, F32, kind="ExternalInput").ap()
    out = nc.dram_tensor("out_0", (BATCH, L, D), F32, kind="ExternalOutput").ap()
    fusion_kernel(nc, aps, out)
    r = run_bass_kernel_spmd(nc, [arrays], core_ids=[0])
    return r.results[0]["out_0"]
```
